# Optimizing a Trainium2 kernel written in Bass

```python
import numpy as np
import jax
import jax.numpy as jnp

def _softmax(x, axis=-1):
    return jax.nn.softmax(x, axis=axis)

def _gelu(x):
    return jax.nn.gelu(x, approximate=True)

def _silu(x):
    return jax.nn.silu(x)

def _sigmoid(x):
    return jax.nn.sigmoid(x)

def _layernorm(x, axis=-1, eps=1e-05):
    m = jnp.mean(x, axis=axis, keepdims=True)
    v = jnp.var(x, axis=axis, keepdims=True)
    return (x - m) / jnp.sqrt(v + eps)

def _scatter_add(tgt, idx, src, axis=0):
    return tgt.at[idx].add(src)

def _segment_sum(src, seg, n):
    return jax.ops.segment_sum(src, seg, n)
kernel_name = 'mk_lm_tower_d1_tok_ids1024_r4_47146d'

def setup_inputs(seed: int=0):
    np.random.seed(seed)
    _w = jnp.asarray

    def _rec_inputs():
        import jax
        import jax.numpy as jnp
        _rk = jax.random.key(seed)
        x = jax.random.randint(jax.random.fold_in(_rk, 1), (128, 128), 0, 50193, jnp.int32)
        return x
    x = _rec_inputs()

    def _L0_tok_setup():
        import jax, jax.numpy as jnp
        import numpy as np
        import math
        VOCAB, HIDDEN = (50257, 256)
        BATCH, SEQ = (4, 128)
        BASE_SEQ = 128
        BITS = 8
        EPS = 1e-05

        def _make_base_pe(base_seq, dim):
            pe = np.zeros((base_seq, dim), dtype=np.float32)
            position = np.arange(base_seq, dtype=np.float32)[:, None]
            div_term = np.exp(np.arange(0, dim, 2, dtype=np.float32) * (-math.log(10000.0) / dim))
            pe[:, 0::2] = np.sin(position * div_term)
            pe[:, 1::2] = np.cos(position * div_term)
            return jnp.asarray(pe)
        BASE_PE = _make_base_pe(BASE_SEQ, HIDDEN)

        def _forward(input_ids, weight, gamma, beta):
            qmin = -2.0 ** (BITS - 1)
            qmax = 2.0 ** (BITS - 1) - 1.0
            wmin, wmax = (weight.min(), weight.max())
            scale = (wmax - wmin) / (qmax - qmin)
            zero_point = qmin - wmin / scale
            deq = (jnp.clip(jnp.round(weight / scale + zero_point), qmin, qmax) - zero_point) * scale
            emb = deq[input_ids]
            x = emb + BASE_PE[None, :SEQ, :]
            mu = x.mean(axis=-1, keepdims=True)
            var = jnp.mean(jnp.square(x - mu), axis=-1, keepdims=True)
            return gamma * (x - mu) * jax.lax.rsqrt(var + EPS) + beta
        key = jax.random.key(seed)
        k1, k2 = jax.random.split(key)
        input_ids = jax.random.randint(k1, (BATCH, SEQ), 0, VOCAB, dtype=jnp.int64 if jax.config.jax_enable_x64 else jnp.int32)
        weight = 0.02 * jax.random.normal(k2, (VOCAB, HIDDEN), dtype=jnp.float32)
        weight = weight.at[0].set(0.0)
        gamma = jnp.ones((HIDDEN,), dtype=jnp.float32)
        beta = jnp.zeros((HIDDEN,), dtype=jnp.float32)
        return {'input_ids': input_ids, 'weight': weight, 'gamma': gamma, 'beta': beta}
    _L0_tok_all = _L0_tok_setup()
    _L0_tok_in = {k: v for k, v in _L0_tok_all.items() if k in ('weight', 'gamma', 'beta')}
    del _L0_tok_all

    def _L0_attn_setup():
        import jax, jax.numpy as jnp
        import numpy as np
        D_MODEL = 256
        N_HEADS = 16
        D_K = D_MODEL // N_HEADS
        SEQ = 1024
        BATCH = 2
        LOCAL_WINDOW = 128
        SCALE = 1.0 / float(np.sqrt(D_K))
        INIT = 1.0 / float(np.sqrt(D_MODEL))

        def _local_mask(seq_len: int) -> jnp.ndarray:
            i = jnp.arange(seq_len)[:, None]
            j = jnp.arange(seq_len)[None, :]
            return (j <= i) & (j >= i - LOCAL_WINDOW)
        key = jax.random.key(seed)
        ks = jax.random.split(key, 9)
        mk = lambda k: jax.random.normal(k, (D_MODEL, D_MODEL), dtype=jnp.float32) * INIT
        return {'x': jax.random.normal(ks[0], (BATCH, SEQ, D_MODEL), dtype=jnp.float32), 'Wq': mk(ks[1]), 'bq': jnp.zeros((D_MODEL,), jnp.float32), 'Wk': mk(ks[2]), 'bk': jnp.zeros((D_MODEL,), jnp.float32), 'Wv': mk(ks[3]), 'bv': jnp.zeros((D_MODEL,), jnp.float32), 'Wo': mk(ks[4]), 'bo': jnp.zeros((D_MODEL,), jnp.float32)}
    _L0_attn_all = _L0_attn_setup()
    _L0_attn_in = {k: v for k, v in _L0_attn_all.items() if k in ('Wq', 'bq', 'Wk', 'bk', 'Wv', 'bv', 'Wo', 'bo')}
    del _L0_attn_all

    def _L0_ffn_setup():
        import jax, jax.numpy as jnp
        import numpy as np
        TOP_K = 6

        def _glu_mlp(x, wg, wu, wd):
            return jax.nn.silu(x @ wg) * (x @ wu) @ wd
        key = jax.random.key(seed)
        ks = jax.random.split(key, 8)
        B, S, D, E, F, FS = (2, 512, 256, 8, 128, 256)
        sc = 0.02
        return {'hidden_states': jax.random.normal(ks[0], (B, S, D), jnp.float32), 'router_w': jax.random.normal(ks[1], (D, E), jnp.float32) * sc, 'w_gate': jax.random.normal(ks[2], (E, D, F), jnp.float32) * sc, 'w_up': jax.random.normal(ks[3], (E, D, F), jnp.float32) * sc, 'w_down': jax.random.normal(ks[4], (E, F, D), jnp.float32) * sc, 'ws_gate': jax.random.normal(ks[5], (D, FS), jnp.float32) * sc, 'ws_up': jax.random.normal(ks[6], (D, FS), jnp.float32) * sc, 'ws_down': jax.random.normal(ks[7], (FS, D), jnp.float32) * sc}
    _L0_ffn_all = _L0_ffn_setup()
    _L0_ffn_in = {k: v for k, v in _L0_ffn_all.items() if k in ('router_w', 'w_gate', 'w_up', 'w_down', 'ws_gate', 'ws_up', 'ws_down')}
    del _L0_ffn_all
    return {'x': x, 'L0_tok_weight': _L0_tok_in['weight'], 'L0_tok_gamma': _L0_tok_in['gamma'], 'L0_tok_beta': _L0_tok_in['beta'], 'L0_attn_Wq': _L0_attn_in['Wq'], 'L0_attn_bq': _L0_attn_in['bq'], 'L0_attn_Wk': _L0_attn_in['Wk'], 'L0_attn_bk': _L0_attn_in['bk'], 'L0_attn_Wv': _L0_attn_in['Wv'], 'L0_attn_bv': _L0_attn_in['bv'], 'L0_attn_Wo': _L0_attn_in['Wo'], 'L0_attn_bo': _L0_attn_in['bo'], 'L0_ffn_router_w': _L0_ffn_in['router_w'], 'L0_ffn_w_gate': _L0_ffn_in['w_gate'], 'L0_ffn_w_up': _L0_ffn_in['w_up'], 'L0_ffn_w_down': _L0_ffn_in['w_down'], 'L0_ffn_ws_gate': _L0_ffn_in['ws_gate'], 'L0_ffn_ws_up': _L0_ffn_in['ws_up'], 'L0_ffn_ws_down': _L0_ffn_in['ws_down']}

def reference(x, L0_tok_weight, L0_tok_gamma, L0_tok_beta, L0_attn_Wq, L0_attn_bq, L0_attn_Wk, L0_attn_bk, L0_attn_Wv, L0_attn_bv, L0_attn_Wo, L0_attn_bo, L0_ffn_router_w, L0_ffn_w_gate, L0_ffn_w_up, L0_ffn_w_down, L0_ffn_ws_gate, L0_ffn_ws_up, L0_ffn_ws_down):
    import jax
    import jax.numpy as jnp

    def _L0_tok_ref(input_ids, weight, gamma, beta):
        import jax, jax.numpy as jnp
        import numpy as np
        import math
        VOCAB, HIDDEN = (50257, 256)
        BATCH, SEQ = (4, 128)
        BASE_SEQ = 128
        BITS = 8
        EPS = 1e-05

        def _make_base_pe(base_seq, dim):
            pe = np.zeros((base_seq, dim), dtype=np.float32)
            position = np.arange(base_seq, dtype=np.float32)[:, None]
            div_term = np.exp(np.arange(0, dim, 2, dtype=np.float32) * (-math.log(10000.0) / dim))
            pe[:, 0::2] = np.sin(position * div_term)
            pe[:, 1::2] = np.cos(position * div_term)
            return jnp.asarray(pe)
        BASE_PE = _make_base_pe(BASE_SEQ, HIDDEN)

        def _forward(input_ids, weight, gamma, beta):
            qmin = -2.0 ** (BITS - 1)
            qmax = 2.0 ** (BITS - 1) - 1.0
            wmin, wmax = (weight.min(), weight.max())
            scale = (wmax - wmin) / (qmax - qmin)
            zero_point = qmin - wmin / scale
            deq = (jnp.clip(jnp.round(weight / scale + zero_point), qmin, qmax) - zero_point) * scale
            emb = deq[input_ids]
            x = emb + BASE_PE[None, :SEQ, :]
            mu = x.mean(axis=-1, keepdims=True)
            var = jnp.mean(jnp.square(x - mu), axis=-1, keepdims=True)
            return gamma * (x - mu) * jax.lax.rsqrt(var + EPS) + beta
        return _forward(input_ids, weight, gamma, beta)

    def _L0_attn_ref(x, Wq, bq, Wk, bk, Wv, bv, Wo, bo):
        import jax, jax.numpy as jnp
        import numpy as np
        D_MODEL = 256
        N_HEADS = 16
        D_K = D_MODEL // N_HEADS
        SEQ = 1024
        BATCH = 2
        LOCAL_WINDOW = 128
        SCALE = 1.0 / float(np.sqrt(D_K))
        INIT = 1.0 / float(np.sqrt(D_MODEL))

        def _local_mask(seq_len: int) -> jnp.ndarray:
            i = jnp.arange(seq_len)[:, None]
            j = jnp.arange(seq_len)[None, :]
            return (j <= i) & (j >= i - LOCAL_WINDOW)
        B, S, _ = x.shape
        q = (x @ Wq.T + bq).reshape(B, S, N_HEADS, D_K)
        k = (x @ Wk.T + bk).reshape(B, S, N_HEADS, D_K)
        v = (x @ Wv.T + bv).reshape(B, S, N_HEADS, D_K)
        scores = jnp.einsum('bqhd,bkhd->bhqk', q, k) * SCALE
        mask = _local_mask(S)[None, None]
        scores = jnp.where(mask, scores, jnp.float32(-10000.0))
        attn = jax.nn.softmax(scores, axis=-1) + jnp.float32(1e-09)
        ctx = jnp.einsum('bhqk,bkhd->bqhd', attn, v).reshape(B, S, D_MODEL)
        return ctx @ Wo.T + bo

    def _L0_ffn_ref(hidden_states, router_w, w_gate, w_up, w_down, ws_gate, ws_up, ws_down):
        import jax, jax.numpy as jnp
        import numpy as np
        TOP_K = 6

        def _glu_mlp(x, wg, wu, wd):
            return jax.nn.silu(x @ wg) * (x @ wu) @ wd
        B, S, D = hidden_states.shape
        x = hidden_states.reshape(-1, D)
        scores = jax.nn.softmax(x @ router_w, axis=-1)
        topk_w, topk_idx = jax.lax.top_k(scores, TOP_K)
        g = jnp.einsum('td,edf->etf', x, w_gate)
        u = jnp.einsum('td,edf->etf', x, w_up)
        f_all = jnp.einsum('etf,efd->ted', jax.nn.silu(g) * u, w_down)
        picked = jnp.take_along_axis(f_all, topk_idx[:, :, None], axis=1)
        y = jnp.sum(picked * topk_w[:, :, None], axis=1).reshape(B, S, D)
        y = y + _glu_mlp(hidden_states, ws_gate, ws_up, ws_down)
        return y
    h = _L0_tok_ref(x, L0_tok_weight, L0_tok_gamma, L0_tok_beta)
    h = h + _L0_attn_ref(_layernorm(h, axis=-1), L0_attn_Wq, L0_attn_bq, L0_attn_Wk, L0_attn_bk, L0_attn_Wv, L0_attn_bv, L0_attn_Wo, L0_attn_bo)
    h = h + _L0_ffn_ref(_layernorm(h, axis=-1), L0_ffn_router_w, L0_ffn_w_gate, L0_ffn_w_up, L0_ffn_w_down, L0_ffn_ws_gate, L0_ffn_ws_up, L0_ffn_ws_down)
    return h

_drawn_inputs = setup_inputs


def setup_inputs(seed=0):
    import zlib

    import numpy as np

    out = dict(_drawn_inputs(seed))
    spreads = {'L0_tok_gamma': (1.0, 0.2),
     'L0_tok_beta': (0.0, 0.1),
     'L0_attn_bq': (0.0, 0.706),
     'L0_attn_bk': (0.0, 0.8),
     'L0_attn_bv': (0.0, 0.1),
     'L0_attn_bo': (0.0, 0.1)}
    factors = {'L0_ffn_router_w': 8.0,
     'L0_ffn_w_gate': 8.0,
     'L0_ffn_w_up': 8.0,
     'L0_ffn_w_down': 8.0,
     'L0_ffn_ws_gate': 4.213,
     'L0_ffn_ws_up': 4.509,
     'L0_ffn_ws_down': 4.447}
    for name, (base, spread) in spreads.items():
        noise = np.random.default_rng([zlib.crc32(name.encode()), seed]).standard_normal(out[name].shape)
        drawn = base * np.exp(spread * noise) if base else spread * noise
        out[name] = jnp.asarray(drawn.astype(out[name].dtype))
    for name, factor in factors.items():
        out[name] = (out[name] * factor).astype(out[name].dtype)
    return out
```

```python
from contextlib import ExitStack

import numpy as np

import concourse.bass as bass
from concourse import mybir

F32 = mybir.dt.float32
BF16 = mybir.dt.bfloat16
I32 = mybir.dt.int32
ALU = mybir.AluOpType
ACT = mybir.ActivationFunctionType
AX = mybir.AxisListType
RED = bass.bass_isa.ReduceOp

P = 128
SEQ = 128
D = 256
KT = D // P
GS = 2
GT = GS * SEQ
HEADS = 16
DK = D // HEADS
HT = HEADS // KT
QUADS = HEADS // 4
STEPS = GS * QUADS
E = 8
TOP_K = 6
FS = 256
UNITS = FS // P + E
SHARED = FS // P
HBUF = 5
EPS = 1e-5
QMIN, QMAX = -128.0, 127.0
ROUND = 1.5 * 2.0 ** 23
MASKED = -1e30
ATTN_EPS = 1e-9
PARTS = 3

GU_SLOT = {4: [0], 5: [1], 6: [2], 8: [3], 9: [4], 10: [5], 12: [6], 13: [7], 14: [8], 15: [9]}
SLOTS = 17


def at(g, per_group, k):
    return g * per_group + k


def later(g):
    return not (isinstance(g, int) and g == 0)


def build(nc, ids, table, base_pe, gamma, beta, wq, bq, wk, bk, wv, bv, wo, bo,
          router, gate, up, down, s_gate, s_up, s_down, ident, mask, pick, sel, out):
    n_rows = table.shape[0]
    batch = ids.shape[1]
    groups = batch // GS
    cols = n_rows * D // P
    n_chunk = 29
    assert cols % n_chunk == 0 and batch % GS == 0
    chunk = cols // n_chunk
    RING = 4
    flat = table.rearrange("r d -> (r d)").rearrange("(p c) -> p c", p=P)

    def held(eng, k):
        eng.sem_inc(waits_over[k], 1)

    with ExitStack() as ctx:
        def sb(name, shape, dt=F32):
            return ctx.enter_context(nc.sbuf_tensor(name, shape, dt))

        def bank(name):
            return ctx.enter_context(nc.psum_tensor(name, [P, 512], F32))

        def sem(name):
            return ctx.enter_context(nc.semaphore(name))

        wq_s, wk_s, wv_s, wo_s = (sb(n, [P, KT, D]) for n in ("wq_s", "wk_s", "wv_s", "wo_s"))
        gu_w = sb("gu_w", [P, UNITS, 2, KT, P])
        dn_w = sb("dn_w", [P, UNITS, D])
        rt_w = sb("rt_w", [P, KT, E])
        bq_s, bk_s = sb("bq_s", [P, KT]), sb("bk_s", [P, KT])
        bv_s, bo_s, gamma_s, beta_s = (sb(n, [P, D]) for n in ("bv_s", "bo_s", "gamma_s", "beta_s"))
        pe_s = sb("pe_s", [P, D])
        ident_f = sb("ident_f", [P, P])
        ident_b = sb("ident_b", [P, P], BF16)
        mask_f = sb("mask_f", [P, 4, P])
        mask_b = sb("mask_b", [P, 4, P], BF16)
        pick_f = sb("pick_f", [HEADS, KT, P])
        sel_f = sb("sel_f", [PARTS * E, E, P])
        sel_b = sb("sel_b", [PARTS * E, E, P], BF16)
        eps_col = sb("eps_col", [P, 1])
        half_pow = sb("half_pow", [P, GS])
        ids_s = sb("ids_s", [P, batch], I32)
        ring = sb("ring", [P, RING, chunk])
        lows, highs = sb("lows", [P, n_chunk]), sb("highs", [P, n_chunk])
        ext, ext_all = sb("ext", [P, 2]), sb("ext_all", [P, 2])
        span, scale, inv, wr, zp = (sb(n, [P, 1]) for n in ("span", "scale", "inv", "wr", "zp"))
        gi = sb("gi", [P, GS], I32)
        raw, xe, xn, h, z, hb = (sb(n, [P, GS, D]) for n in ("raw", "xe", "xn", "h", "z", "hb"))
        st1, st2, st3 = (sb(n, [P, GS, 6]) for n in ("st1", "st2", "st3"))
        mv1, mv2, mv3 = (sb(n, [P, GS, 2]) for n in ("mv1", "mv2", "mv3"))
        ve1, ve2, ve3 = (sb(n, [P, GS]) for n in ("ve1", "ve2", "ve3"))
        rs1, rs2, rs3 = (sb(n, [P, GS]) for n in ("rs1", "rs2", "rs3"))
        zT, qT = (sb(n, [P, KT, GT]) for n in ("zT", "qT"))
        kT = sb("kT", [P, GS, KT, SEQ])
        kbd = sb("kbd", [P, GS, KT, HT, SEQ])
        vpad = sb("vpad", [P, GS, HEADS, 2 * DK])
        v_s = sb("v_s", [P, GS, D])
        vs = sb("vs", [P, GS * KT])
        nm = sb("nm", [P, STEPS, 4])
        sm, rsm = sb("sm", [P, GS, HEADS]), sb("rsm", [P, GS, HEADS])
        pr = sb("pr", [P, 2, 4, SEQ])
        pT = sb("pT", [P, 2, 4, SEQ])
        rT = sb("rT", [HEADS, GS, SEQ])
        cu = sb("cu", [P, GS, KT * SEQ])
        cx = sb("cx", [P, GS, KT, SEQ])
        h1, z2, res = (sb(n, [P, GS, D]) for n in ("h1", "z2", "res"))
        z2T = sb("z2T", [P, KT, GT])
        lmax, esum, erec = sb("lmax", [P, GS]), sb("esum", [P, GS]), sb("erec", [P, GS])
        ex = sb("ex", [P, GS, E])
        p10 = sb("p10", [P, GS, E + 2])
        left = sb("left", [P, GS, E + 2])
        top = sb("top", [P, GS, 8])
        strike = sb("strike", [P, GS, 2])
        wts, wr1, wr2 = (sb(n, [P, GS, E]) for n in ("wts", "wr1", "wr2"))
        wparts = sb("wparts", [P, GS, PARTS, E], BF16)
        wT = sb("wT", [PARTS * E, GT], BF16)
        wbc = sb("wbc", [P, E, GT])
        tn, ga, gb = sb("tn", [P, 2, GT]), sb("ga", [P, 2, GT]), sb("gb", [P, 2, GT])
        hh = sb("hh", [P, HBUF, GT])
        ob = sb("ob", [P, GS, D])

        b_s = [bank("b_s0"), bank("b_s1")]
        b_pt = bank("b_pt")
        b_ct = bank("b_ct")
        b_m = bank("b_m")
        b_g = [bank("b_g0"), bank("b_g1")]
        b_y = bank("b_y")

        w_load, v_load = sem("w_load"), sem("v_load")
        waits_over = [sem("pool_waits_over"), sem("dve_waits_over")]
        chunk_in = [sem(f"chunk_in{j}") for j in range(RING)]
        chunk_used, range_step, range_all = sem("chunk_used"), sem("range_step"), sem("range_all")
        consts = sem("consts")
        idx_copied, gathered = sem("idx_copied"), sem("gathered")
        quant, stats1, mean1, var1, rstd1, normed1, scaled1, h_ready = (sem(n) for n in (
            "quant", "stats1", "mean1", "var1", "rstd1", "normed1", "scaled1", "h_ready"))
        stats2, mean2, var2, rstd2, z_ready, hb_ready = (sem(n) for n in (
            "stats2", "mean2", "var2", "rstd2", "z_ready", "hb_ready"))
        z_posed, zT_ready, k_done, k_ready, kbd_ready, q_done, q_ready = (sem(n) for n in (
            "z_posed", "zT_ready", "k_done", "k_ready", "kbd_ready", "q_done", "q_ready"))
        v_done, v_ready, vpad_ready, vs_done, vs_ready = (sem(n) for n in (
            "v_done", "v_ready", "vpad_ready", "vs_done", "vs_ready"))
        s_done, max_ready, exp_done, p_posed, pT_ready, pv_done = (sem(n) for n in (
            "s_done", "max_ready", "exp_done", "p_posed", "pT_ready", "pv_done"))
        r_ready, r_posed, rT_ready, rbc_done, cu_ready, c_mul, c_ready, o_done = (sem(n) for n in (
            "r_ready", "r_posed", "rT_ready", "rbc_done", "cu_ready", "c_mul", "c_ready", "o_done"))
        h1_ready, stats3, mean3, var3, rstd3, z2_ready, res_ready = (sem(n) for n in (
            "h1_ready", "stats3", "mean3", "var3", "rstd3", "z2_ready", "res_ready"))
        z2_posed, z2T_ready, l_done, l_max, r_exp, route = (sem(n) for n in (
            "z2_posed", "z2T_ready", "l_done", "l_max", "r_exp", "route"))
        w_posed, wT_ready, wbc_done, wbc_ready = (sem(n) for n in ("w_posed", "wT_ready", "wbc_done", "wbc_ready"))
        gu_done, tanh_done, a_done, b_done, hw_done, d_done, out_ready, out_sent = (sem(n) for n in (
            "gu_done", "tanh_done", "a_done", "b_done", "hw_done", "d_done", "out_ready", "out_sent"))

        ROUTE = 14
        KBD = 16 * HT
        W_LOADS = 16 * 23

        def bodies(step, eng):
            step(0, 1, 0, None)
            step(1, 2, 1, 0)
            with eng.Fori(2, groups - 2) as i:
                step(i, i + 1, i, i - 1)
            step(groups - 2, groups - 1, groups - 2, groups - 3)
            step(groups - 1, None, groups - 1, groups - 2)
            step(groups, None, None, groups - 1)

        block = ctx.enter_context(nc.Block())

        @block.sync
        def _(sp):
            def load_chunk(c, j):
                sp.dma_start(ring[:, j, :], flat[:, bass.ds(c * chunk, chunk)]).then_inc(chunk_in[j], 16)

            for j in range(RING):
                load_chunk(j, j)
            with sp.Fori(1, n_chunk // RING) as r:
                for j in range(RING):
                    sp.wait_ge(chunk_used, r * 2 * RING + (2 * (j + 1) - 2 * RING))
                    load_chunk(r * RING + j, j)
            for c in range(n_chunk // RING * RING, n_chunk):
                sp.wait_ge(chunk_used, 2 * (c - RING + 1))
                load_chunk(c, c % RING)

            def step(i, e, a, f):
                if a is not None:
                    sp.wait_ge(k_ready, at(a, KT, KT))
                    if later(a):
                        sp.wait_ge(s_done, at(a - 1, STEPS, STEPS))
                    for hd in range(HT):
                        rows = slice(DK * hd, DK * hd + DK)
                        sp.dma_start(kbd[rows, :, :, hd, :],
                                     kT[rows]).then_inc(kbd_ready, 16)
                if f is not None:
                    sp.wait_ge(out_ready, at(f, 1, 1))
                    sp.dma_start(out[bass.ds(f * GS, GS)].rearrange("s p d -> p s d"), ob[:]).then_inc(out_sent, 16)

            bodies(step, sp)
            sp.wait_ge(out_sent, 16 * groups)

        @block.gpsimd
        def _(pool):
            pool.memset(eps_col[:], ATTN_EPS).then_inc(consts, 1)
            pool.memset(half_pow[:], -0.5).then_inc(consts, 1)
            pool.memset(strike[:, :, 0:1], -1.0).then_inc(consts, 1)
            pool.memset(strike[:, :, 1:2], -2.0).then_inc(consts, 1)
            pool.memset(p10[:, :, E:E + 1], -1.0).then_inc(consts, 1)
            pool.memset(p10[:, :, E + 1:E + 2], -2.0).then_inc(consts, 1)
            pool.memset(kbd[:], 0.0).then_inc(consts, 1)
            pool.memset(vpad[:], 0.0).then_inc(consts, 1)
            pool.wait_ge(w_load, W_LOADS)

            def gather(g):
                if later(g):
                    pool.wait_ge(gathered, at(g - 1, 32, 32))
                    pool.wait_ge(quant, at(g - 1, 4, 1))
                held(pool, 0)
                pool.tensor_copy(gi[:], ids_s[:, bass.ds(g * GS, GS)]).then_inc(idx_copied, 1)
                pool.wait_ge(idx_copied, at(g, 1, 1))
                for s in range(GS):
                    held(pool, 0)
                    pool.indirect_dma_start(
                        raw[:, s, :], None, table,
                        bass.IndirectOffsetOnAxis(ap=gi[:, s:s + 1].bitcast(mybir.dt.uint32), axis=0)).then_inc(gathered, 16)

            def rstd(g, mean, k, mv, ve, rs, var, done, per, s):
                pool.wait_ge(mean, at(g, GS, k))
                held(pool, 0)
                pool.tensor_scalar(ve[:, s], mv[:, s, 1], EPS, 1.0, ALU.add, ALU.mult).then_inc(var, 1)
                pool.wait_ge(var, at(g, per, k * per // GS))
                pool.tensor_tensor(rs[:, s], ve[:, s], half_pow[:, s], ALU.pow).then_inc(done, 1)

            def scale_h(g):
                pool.wait_ge(normed1, at(g, GS, GS))
                if later(g):
                    pool.wait_ge(z_ready, at(g - 1, GS, GS))
                pool.tensor_tensor(h[:], xn[:], gamma_s[:].unsqueeze(1).broadcast_to([P, GS, D]), ALU.mult).then_inc(scaled1, 1)
                pool.wait_ge(scaled1, at(g, 1, 1))
                pool.tensor_tensor(h[:], h[:], beta_s[:].unsqueeze(1).broadcast_to([P, GS, D]), ALU.add).then_inc(h_ready, 1)

            def residual(g):
                pool.wait_ge(h_ready, at(g, 1, 1))
                if later(g):
                    pool.wait_ge(h1_ready, at(g - 1, GS, GS))
                pool.tensor_tensor(hb[:], h[:], bo_s[:].unsqueeze(1).broadcast_to([P, GS, D]), ALU.add).then_inc(hb_ready, 1)

            def keep(f):
                pool.wait_ge(h1_ready, at(f, GS, GS))
                if later(f):
                    pool.wait_ge(out_ready, at(f - 1, 1, 1))
                held(pool, 0)
                pool.tensor_copy(res[:], h1[:]).then_inc(res_ready, 1)

            def pad_values(a):
                pool.wait_ge(v_ready, at(a, 1, 1))
                if later(a):
                    pool.wait_ge(pv_done, at(a - 1, STEPS, STEPS))
                for o in range(2):
                    held(pool, 0)
                    pool.tensor_copy(vpad[:].rearrange("p s (j o) c -> p s j o c", o=2)[:, :, :, o, DK * o:DK * o + DK],
                                     v_s[:].rearrange("p s (j o d) -> p s j o d", o=2, d=DK)[:, :, :, o, :]
                                     ).then_inc(vpad_ready, 1)

            def add_vs(a, s):
                pool.wait_ge(c_mul, at(a, GS, s + 1))
                pool.wait_ge(vs_ready, at(a, 1, 1))
                for t in range(KT):
                    held(pool, 0)
                    pool.tensor_scalar(cx[:, s, t, :], cx[:, s, t, :], vs[:, s * KT + t:s * KT + t + 1], 1.0,
                                       ALU.add, ALU.mult).then_inc(c_ready, 1)

            def weigh(f, u):
                e = u - SHARED
                pool.wait_ge(b_done, at(f, UNITS, u + 1))
                pool.wait_ge(wbc_ready, at(f, E // 2, e // 2 + 1))
                if u >= HBUF:
                    pool.wait_ge(d_done, at(f, UNITS, u - HBUF + 1))
                elif later(f):
                    pool.wait_ge(d_done, at(f - 1, UNITS, u - HBUF + UNITS + 1))
                pool.tensor_tensor(hh[:, u % HBUF, :], gb[:, u % 2, :], wbc[:, e, :], ALU.mult).then_inc(hw_done, 1)

            def embed_a(e):
                rstd(e, mean1, GS, mv1, ve1, rs1, var1, rstd1, 1, slice(0, GS))
                scale_h(e)

            def embed_b(e):
                rstd(e, mean2, GS, mv2, ve2, rs2, var2, rstd2, 1, slice(0, GS))

            def step(i, e, a, f):
                for t in range(SLOTS):
                    if t == 0:
                        if a is not None:
                            residual(a)
                        if f is not None:
                            keep(f)
                        if e is not None:
                            embed_a(e)
                    if t == 3 and a is not None:
                        pad_values(a)
                    if t == 4 and e is not None:
                        embed_b(e)
                        if isinstance(e, int):
                            if e + 1 < groups:
                                gather(e + 1)
                        else:
                            gather(e + 1)
                    if a is not None and t in (12, 15):
                        add_vs(a, (t - 12) // 3)
                    if f is not None:
                        for u in GU_SLOT.get(t, []):
                            if u >= SHARED:
                                weigh(f, u)
                    if a is not None and t in (13, 16):
                        s = (t - 13) // 3
                        rstd(a, mean3, s + 1, mv3, ve3, rs3, var3, rstd3, GS, slice(s, s + 1))

            pool.wait_ge(range_step, 3)
            pool.partition_all_reduce(ext_all[:], ext[:], P, RED.max).then_inc(range_all, 1)
            gather(0)
            embed_a(0)
            embed_b(0)
            gather(1)
            bodies(step, pool)

        @block.scalar
        def _(act):
            def load(dst, src, s=w_load):
                act.dma_start(dst, src).then_inc(s, 16)

            for dst, src in ((wq_s, wq), (wk_s, wk), (wv_s, wv), (wo_s, wo), (rt_w, router)):
                load(dst[:], src.rearrange("(t p) n -> p t n", p=P))
            for dst, src in ((bq_s, bq), (bk_s, bk)):
                load(dst[:], src)
            for dst, src in ((bv_s, bv), (bo_s, bo), (gamma_s, gamma), (beta_s, beta)):
                load(dst[:], src.partition_broadcast(P))
            load(pe_s[:], base_pe)
            load(ident_f[:], ident)
            load(mask_f[:], mask.unsqueeze(1).broadcast_to([P, 4, P]))
            load(pick_f[:], pick)
            load(sel_f[:], sel)
            load(ids_s[:], ids)
            load(dn_w[:, 0:SHARED, :], s_down.rearrange("(u p) d -> p u d", p=P))
            load(dn_w[:, SHARED:UNITS, :], down.rearrange("e p d -> p e d"))
            for k, (ex_w, sh_w) in enumerate(((gate, s_gate), (up, s_up))):
                load(gu_w[:, 0:SHARED, k, 0, :], sh_w.rearrange("(t p) (u f) -> t p u f", p=P, f=P)[0])
                load(gu_w[:, 0:SHARED, k, 1, :], sh_w.rearrange("(t p) (u f) -> t p u f", p=P, f=P)[1])
            for k, ex_w in enumerate((gate, up)):
                for t in range(KT):
                    act.dma_start(gu_w[:, SHARED:UNITS, k, t, :],
                                  ex_w.rearrange("e (t p) f -> t p e f", p=P)[t]).then_inc(v_load, 16)
            act.wait_ge(w_load, W_LOADS)

            def exps(a, q):
                act.wait_ge(max_ready, at(a, STEPS, q + 1))
                if q >= 2:
                    act.wait_ge(p_posed, at(a, STEPS, q - 1))
                elif later(a):
                    act.wait_ge(p_posed, at(a - 1, STEPS, STEPS + q - 1))
                s, c = divmod(q, QUADS)
                for j in range(4):
                    hd = 4 * c + j
                    act.activation(pr[:, q % 2, j, :], b_s[q % 2][:, SEQ * j:SEQ * j + SEQ], ACT.Exp,
                                   bias=nm[:, q, j:j + 1], accum_out=sm[:, s, hd:hd + 1]).then_inc(exp_done, 1)

            def step(i, e, a, f):
                for t in range(SLOTS):
                    if a is not None:
                        if t == 1:
                            act.wait_ge(k_done, at(a, 1, 1))
                            if later(a):
                                act.wait_ge(kbd_ready, at(a - 1, KBD, KBD))
                            for kt in range(KT):
                                act.activation(kT[:, :, kt, :], b_s[0][:, GT * kt:GT * kt + GT].rearrange("p (s n) -> p s n", s=GS),
                                               ACT.Identity,
                                               bias=bk_s[:, kt:kt + 1]).then_inc(k_ready, 1)
                        if 4 <= t < 4 + STEPS:
                            exps(a, t - 4)
                        if t in (10, 13):
                            s = (t - 10) // 3
                            act.wait_ge(r_posed, at(a, GS, s + 1))
                            act.activation(rT[:, s, :], b_m[0:HEADS, 0:SEQ], ACT.Copy).then_inc(rT_ready, 1)
                    if f is not None:
                        if t == 3:
                            act.wait_ge(z2_posed, at(f, 1, 1))
                            act.activation(z2T[:].rearrange("p t n -> p (t n)"), b_m[:], ACT.Copy).then_inc(z2T_ready, 1)
                        if t == 4:
                            act.wait_ge(l_max, at(f, 1, 1))
                            for s in range(GS):
                                act.activation(ex[:, s, :], b_m[:, E * s:E * s + E], ACT.Exp, bias=lmax[:, s:s + 1],
                                               accum_out=esum[:, s:s + 1]).then_inc(r_exp, 1)
                        if t == 5:
                            act.wait_ge(w_posed, at(f, 1, 1))
                            act.activation(wT[:], b_m[0:PARTS * E, 0:GT // 2].bitcast(BF16), ACT.Copy).then_inc(wT_ready, 1)
                        if 6 <= t < 6 + E // 2:
                            j = t - 6
                            act.wait_ge(wbc_done, at(f, E // 2, j + 1))
                            if later(f):
                                act.wait_ge(hw_done, at(f - 1, E, 2 * j + 2))
                            act.activation(wbc[:, 2 * j:2 * j + 2, :].rearrange("p e n -> p (e n)"), b_m[:],
                                           ACT.Copy).then_inc(wbc_ready, 1)
                        for u in GU_SLOT.get(t, []):
                            act.wait_ge(gu_done, at(f, UNITS, u + 1))
                            act.activation(tn[:, u % 2, :], b_g[u % 2][:, 0:GT], ACT.Tanh, scale=0.5).then_inc(tanh_done, 1)
                    if a is not None and t in (9, 13):
                        s = (t - 9) // 4
                        act.wait_ge(pv_done, at(a, STEPS, QUADS * (s + 1)))
                        if later(a):
                            act.wait_ge(c_mul, at(a - 1, GS, s + 1))
                        act.activation(cu[:, s, :], b_ct[:, D * s:D * s + D], ACT.Copy).then_inc(cu_ready, 1)

            bodies(step, act)

        @block.vector
        def _(dve):
            dve.wait_ge(w_load, W_LOADS)
            dve.tensor_copy(ident_b[:], ident_f[:]).then_inc(consts, 1)
            dve.tensor_copy(mask_b[:], mask_f[:]).then_inc(consts, 1)
            dve.tensor_copy(sel_b[:], sel_f[:]).then_inc(consts, 1)

            def extremes(c, j, seen):
                dve.wait_ge(chunk_in[j], seen)
                dve.tensor_reduce(highs[:, bass.ds(c, 1)], ring[:, j, :], AX.X, ALU.max).then_inc(chunk_used, 1)
                dve.tensor_reduce(lows[:, bass.ds(c, 1)], ring[:, j, :], AX.X, ALU.min).then_inc(chunk_used, 1)

            with dve.Fori(0, n_chunk // RING) as r:
                for j in range(RING):
                    extremes(r * RING + j, j, r * 16 + 16)
            for c in range(n_chunk // RING * RING, n_chunk):
                extremes(c, c % RING, 16 * (c // RING + 1))
            dve.wait_ge(chunk_used, 2 * n_chunk)
            dve.tensor_reduce(ext[:, 0:1], highs[:], AX.X, ALU.max).then_inc(range_step, 1)
            dve.tensor_reduce(ext[:, 1:2], lows[:], AX.X, ALU.min).then_inc(range_step, 1)
            dve.wait_ge(range_step, 2)
            dve.tensor_scalar(ext[:, 1:2], ext[:, 1:2], -1.0, None, ALU.mult).then_inc(range_step, 1)
            dve.wait_ge(range_all, 1)
            dve.tensor_tensor(span[:], ext_all[:, 0:1], ext_all[:, 1:2], ALU.add).then_inc(range_step, 1)
            dve.wait_ge(range_step, 4)
            dve.tensor_scalar(scale[:], span[:], 1.0 / (QMAX - QMIN), None, ALU.mult).then_inc(range_step, 1)
            dve.wait_ge(range_step, 5)
            dve.reciprocal(inv[:], scale[:]).then_inc(range_step, 1)
            dve.wait_ge(range_step, 6)
            dve.tensor_tensor(wr[:], ext_all[:, 1:2], inv[:], ALU.mult).then_inc(range_step, 1)
            dve.wait_ge(range_step, 7)
            dve.tensor_scalar(zp[:], wr[:], QMIN, None, ALU.add).then_inc(range_step, 1)
            dve.wait_ge(range_step, 8)
            dve.wait_ge(consts, 11)

            def quantise(g):
                dve.wait_ge(gathered, at(g, 32, 32))
                dve.tensor_scalar(xe[:], raw[:], inv[:], zp[:], ALU.mult, ALU.add).then_inc(quant, 1)
                dve.wait_ge(quant, at(g, 4, 1))
                dve.tensor_scalar(xe[:], xe[:], QMAX, QMIN, ALU.min, ALU.max).then_inc(quant, 1)
                dve.wait_ge(quant, at(g, 4, 2))
                dve.tensor_scalar(xe[:], xe[:], ROUND, ROUND, ALU.add, ALU.subtract).then_inc(quant, 1)
                dve.wait_ge(quant, at(g, 4, 3))
                dve.tensor_scalar(xe[:], xe[:], zp[:], scale[:], ALU.subtract, ALU.mult).then_inc(quant, 1)
                dve.wait_ge(quant, at(g, 4, 4))
                dve.tensor_tensor(xe[:], xe[:], pe_s[:].unsqueeze(1).broadcast_to([P, GS, D]), ALU.add).then_inc(stats1, 1)
                dve.wait_ge(stats1, at(g, 1 + GS, 1))
                for s in range(GS):
                    dve.bn_stats(st1[:, s, :], xe[:, s, :]).then_inc(stats1, 1)
                for s in range(GS):
                    dve.wait_ge(stats1, at(g, 1 + GS, s + 2))
                    held(dve, 1)
                    dve.bn_aggr(mv1[:, s, :], st1[:, s, :]).then_inc(mean1, 1)

            def normalise(g, x, mv, rs, y, rstd, k, per, s, done):
                dve.wait_ge(rstd, at(g, per, k))
                dve.tensor_scalar(y[:, s, :], x[:, s, :], mv[:, s, 0:1], rs[:, s:s + 1], ALU.subtract, ALU.mult).then_inc(done, 1)

            def norm1(g):
                if later(g):
                    dve.wait_ge(scaled1, at(g - 1, 1, 1))
                for s in range(GS):
                    normalise(g, xe, mv1, rs1, xn, rstd1, 1, 1, s, normed1)

            def stat2(g):
                dve.wait_ge(h_ready, at(g, 1, 1))
                for s in range(GS):
                    dve.bn_stats(st2[:, s, :], h[:, s, :]).then_inc(stats2, 1)
                for s in range(GS):
                    dve.wait_ge(stats2, at(g, GS, s + 1))
                    held(dve, 1)
                    dve.bn_aggr(mv2[:, s, :], st2[:, s, :]).then_inc(mean2, 1)

            def norm2(g):
                if later(g):
                    dve.wait_ge(z_posed, at(g - 1, 1, 1))
                for s in range(GS):
                    normalise(g, h, mv2, rs2, z, rstd2, 1, 1, s, z_ready)

            def max_of(a, q):
                dve.wait_ge(s_done, at(a, STEPS, q + 1))
                dve.tensor_reduce(nm[:, q, :], b_s[q % 2][:].rearrange("p (j n) -> p j n", j=4), AX.X, ALU.max,
                                  negate=True).then_inc(max_ready, 1)

            def keep_pT(a, q):
                dve.wait_ge(p_posed, at(a, STEPS, q + 1))
                if q >= 2:
                    dve.wait_ge(pv_done, at(a, STEPS, q - 1))
                elif later(a):
                    dve.wait_ge(pv_done, at(a - 1, STEPS, STEPS + q - 1))
                dve.tensor_copy(pT[:, q % 2].rearrange("p j n -> p (j n)"), b_pt[:]).then_inc(pT_ready, 1)

            def route_steps(f):
                n = [0]

                def did(ins):
                    n[0] += 1
                    ins.then_inc(route, 1)
                    dve.wait_ge(route, at(f, ROUTE, n[0]))

                dve.wait_ge(r_exp, at(f, GS, GS))
                did(dve.reciprocal(erec[:], esum[:]))
                for s in range(GS):
                    did(dve.tensor_scalar(p10[:, s, 0:E], ex[:, s, :], erec[:, s:s + 1], None, ALU.mult))
                for s in range(GS):
                    held(dve, 1)
                    did(dve.max(top[:, s, :], p10[:, s, 0:E]))
                did(dve.tensor_copy(top[:, :, TOP_K:8], strike[:]))
                for s in range(GS):
                    held(dve, 1)
                    did(dve.match_replace(left[:, s, :], top[:, s, :], p10[:, s, :], 0.0))
                did(dve.tensor_tensor(wts[:], p10[:, :, 0:E], left[:, :, 0:E], ALU.subtract))
                did(dve.tensor_copy(wparts[:, :, 0, :], wts[:]))
                did(dve.tensor_tensor(wr1[:], wts[:], wparts[:, :, 0, :], ALU.subtract))
                did(dve.tensor_copy(wparts[:, :, 1, :], wr1[:]))
                did(dve.tensor_tensor(wr2[:], wr1[:], wparts[:, :, 1, :], ALU.subtract))
                did(dve.tensor_copy(wparts[:, :, 2, :], wr2[:]))
                assert n[0] == ROUTE

            def gated(f, u):
                dve.wait_ge(tanh_done, at(f, UNITS, u + 1))
                dve.scalar_tensor_tensor(ga[:, u % 2, :], tn[:, u % 2, :], 1.0, b_g[u % 2][:, 0:GT],
                                         ALU.add, ALU.mult).then_inc(a_done, 1)
                dve.wait_ge(a_done, at(f, UNITS, u + 1))
                if u < SHARED:
                    if later(f):
                        dve.wait_ge(d_done, at(f - 1, UNITS, UNITS - HBUF + u + 1))
                    dve.scalar_tensor_tensor(hh[:, u, :], ga[:, u % 2, :], 0.5, b_g[u % 2][:, GT:2 * GT],
                                             ALU.mult, ALU.mult).then_inc(b_done, 1)
                else:
                    e = u - SHARED
                    if e >= 2:
                        dve.wait_ge(hw_done, at(f, E, e - 1))
                    elif later(f):
                        dve.wait_ge(hw_done, at(f - 1, E, E + e - 1))
                    dve.tensor_tensor(gb[:, u % 2, :], ga[:, u % 2, :], b_g[u % 2][:, GT:2 * GT], ALU.mult).then_inc(b_done, 1)

            def after_out(a, s):
                dve.wait_ge(o_done, at(a, GS, s + 1))
                dve.wait_ge(hb_ready, at(a, 1, 1))
                if later(a):
                    dve.wait_ge(res_ready, at(a - 1, 1, 1))
                dve.tensor_tensor(h1[:, s, :], b_m[:, 0:D], hb[:, s, :], ALU.add).then_inc(h1_ready, 1)
                dve.wait_ge(h1_ready, at(a, GS, s + 1))
                dve.bn_stats(st3[:, s, :], h1[:, s, :]).then_inc(stats3, 1)
                dve.wait_ge(stats3, at(a, GS, s + 1))
                held(dve, 1)
                dve.bn_aggr(mv3[:, s, :], st3[:, s, :]).then_inc(mean3, 1)

            def norm3(a, s):
                if later(a):
                    dve.wait_ge(z2_posed, at(a - 1, 1, 1))
                normalise(a, h1, mv3, rs3, z2, rstd3, s + 1, GS, s, z2_ready)

            def step(i, e, a, f):
                for t in range(SLOTS):
                    if a is not None:
                        if t in (13, 16):
                            after_out(a, (t - 13) // 3)
                        if t == 0:
                            dve.wait_ge(z_posed, at(a, 1, 1))
                            if later(a):
                                dve.wait_ge(v_done, at(a - 1, 1, 1))
                            dve.tensor_copy(zT[:].rearrange("p t n -> p (t n)"), b_pt[:]).then_inc(zT_ready, 1)
                        if t == 2:
                            dve.wait_ge(q_done, at(a, 1, 1))
                            for kt in range(KT):
                                dve.tensor_scalar(qT[:, kt, :], b_s[1][:, GT * kt:GT * kt + GT], bq_s[:, kt:kt + 1],
                                                  float(DK) ** -0.5, ALU.add, ALU.mult).then_inc(q_ready, 1)
                        if t == 3:
                            dve.wait_ge(v_done, at(a, 1, 1))
                            if later(a):
                                dve.wait_ge(vpad_ready, at(a - 1, 2, 2))
                            dve.tensor_tensor(v_s[:], b_pt[:].rearrange("p (s d) -> p s d", s=GS),
                                              bv_s[:].unsqueeze(1).broadcast_to([P, GS, D]), ALU.add).then_inc(v_ready, 1)
                            dve.wait_ge(vs_done, at(a, 1, 1))
                            dve.tensor_copy(vs[:], b_ct[:, 0:GS * KT]).then_inc(vs_ready, 1)
                        if 4 <= t < 4 + STEPS:
                            max_of(a, t - 4)
                        if 5 <= t < 5 + STEPS:
                            keep_pT(a, t - 5)
                        if t in (9, 12):
                            s = (t - 9) // 3
                            dve.wait_ge(exp_done, at(a, 4 * STEPS, 4 * QUADS * (s + 1)))
                            dve.reciprocal(rsm[:, s, :], sm[:, s, :]).then_inc(r_ready, 1)
                        if t in (12, 15):
                            s = (t - 12) // 3
                            dve.wait_ge(cu_ready, at(a, GS, s + 1))
                            dve.wait_ge(rbc_done, at(a, GS, s + 1))
                            dve.tensor_tensor(cx[:, s].rearrange("p t n -> p (t n)"), cu[:, s, :],
                                              b_m[:, SEQ:SEQ + D], ALU.mult).then_inc(c_mul, 1)
                    if e is not None:
                        if t == 0:
                            quantise(e)
                        if t == 1:
                            norm1(e)
                        if t == 3:
                            stat2(e)
                        if t == 5:
                            norm2(e)
                    if f is not None:
                        if t == 4:
                            dve.wait_ge(l_done, at(f, 1, 1))
                            dve.tensor_reduce(lmax[:], b_m[:, 0:GS * E].rearrange("p (s e) -> p s e", s=GS), AX.X, ALU.max,
                                              negate=True).then_inc(l_max, 1)
                            route_steps(f)
                        for u in GU_SLOT.get(t, []):
                            gated(f, u)
                    if a is not None and t in (14, 16):
                        norm3(a, (t - 14) // 2)
                    if f is not None and t == SLOTS - 1:
                        dve.wait_ge(d_done, at(f, UNITS, UNITS))
                        dve.wait_ge(res_ready, at(f, 1, 1))
                        if later(f):
                            dve.wait_ge(out_sent, at(f - 1, 16, 16))
                        dve.tensor_tensor(ob[:].rearrange("p s d -> p (s d)"), b_y[:], res[:].rearrange("p s d -> p (s d)"),
                                          ALU.add).then_inc(out_ready, 1)

            quantise(0)
            norm1(0)
            stat2(0)
            norm2(0)
            bodies(step, dve)

        @block.tensor
        def _(pe):
            pe.wait_ge(w_load, W_LOADS)
            pe.wait_ge(v_load, 16 * 4)
            pe.wait_ge(consts, 11)

            def pose(x, dst):
                for kt in range(KT):
                    for s in range(GS):
                        m = pe.transpose(dst[:, GT * kt + SEQ * s:GT * kt + SEQ * s + SEQ],
                                         x[:, s, P * kt:P * kt + P], ident_f[:])
                return m

            def project(w, dst):
                for m in range(KT):
                    for kt in range(KT):
                        mm = pe.matmul(dst[:, GT * m:GT * m + GT], w[:, kt, P * m:P * m + P], zT[:, kt, :],
                                       start=(kt == 0), stop=(kt == KT - 1))
                return mm

            def scores(a, q):
                s, c = divmod(q, QUADS)
                t, h0 = c // 2, 4 * (c % 2)
                if q == 0:
                    pe.wait_ge(q_ready, at(a, KT, KT))
                    pe.wait_ge(kbd_ready, at(a, KBD, KBD))
                else:
                    if q >= 2:
                        pe.wait_ge(exp_done, at(a, 4 * STEPS, 4 * (q - 1)))
                pe.matmul(b_s[q % 2][:], ident_b[:], mask_b[:].rearrange("p j n -> p (j n)"), start=True, stop=False)
                pe.matmul(b_s[q % 2][:], qT[:, t, SEQ * s:SEQ * s + SEQ],
                          kbd[:, s, t, h0:h0 + 4, :].rearrange("p j n -> p (j n)"),
                          start=False, stop=True).then_inc(s_done, 1)

            def pose_p(a, q):
                pe.wait_ge(exp_done, at(a, 4 * STEPS, 4 * (q + 1)))
                if q == 0:
                    pe.wait_ge(v_ready, at(a, 1, 1))
                else:
                    pe.wait_ge(pT_ready, at(a, STEPS, q))
                for j in range(4):
                    m = pe.transpose(b_pt[:, SEQ * j:SEQ * j + SEQ], pr[:, q % 2, j, :], ident_f[:])
                m.then_inc(p_posed, 1)

            def weigh_v(a, q):
                s, c = divmod(q, QUADS)
                t = c // 2
                pe.wait_ge(pT_ready, at(a, STEPS, q + 1))
                if q == 0:
                    pe.wait_ge(vs_ready, at(a, 1, 1))
                    pe.wait_ge(vpad_ready, at(a, 2, 2))
                if q == QUADS:
                    pe.wait_ge(cu_ready, at(a, GS, 1))
                for j in (0, 2, 1, 3):
                    hd = 4 * c + j
                    r = hd % HT // 2 * 2 * DK
                    m = pe.matmul(b_ct[r:r + 2 * DK, D * s + SEQ * t:D * s + SEQ * t + SEQ], vpad[:, s, hd, :],
                                  pT[:, q % 2, j, :], start=(j % 2 == 0), stop=(j % 2 == 1))
                m.then_inc(pv_done, 1)

            def gate_up(f, u):
                if u == 0:
                    pe.wait_ge(z2T_ready, at(f, 1, 1))
                if u >= 2:
                    pe.wait_ge(b_done, at(f, UNITS, u - 1))
                elif later(f):
                    pe.wait_ge(b_done, at(f - 1, UNITS, UNITS + u - 1))
                for k in range(2):
                    for kt in range(KT):
                        m = pe.matmul(b_g[u % 2][:, GT * k:GT * k + GT], gu_w[:, u, k, kt, :], z2T[:, kt, :],
                                      start=(kt == 0), stop=(kt == KT - 1))
                m.then_inc(gu_done, 1)

            def down_of(f, u):
                if u < SHARED:
                    pe.wait_ge(b_done, at(f, UNITS, u + 1))
                else:
                    pe.wait_ge(hw_done, at(f, E, u - SHARED + 1))
                if u == 0 and later(f):
                    pe.wait_ge(out_ready, at(f - 1, 1, 1))
                for s in range(GS):
                    m = pe.matmul(b_y[:, D * s:D * s + D], hh[:, u % HBUF, SEQ * s:SEQ * s + SEQ], dn_w[:, u, :],
                                  start=(u == 0 and s == 0), stop=(u == UNITS - 1), skip_group_check=True)
                m.then_inc(d_done, 1)

            def step(i, e, a, f):
                for t in range(SLOTS):
                    if a is not None:
                        if t == 0:
                            pe.wait_ge(z_ready, at(a, GS, GS))
                            if later(a):
                                pe.wait_ge(pT_ready, at(a - 1, STEPS, STEPS))
                            pose(z, b_pt).then_inc(z_posed, 1)
                        if t == 1:
                            pe.wait_ge(zT_ready, at(a, 1, 1))
                            if later(a):
                                pe.wait_ge(exp_done, at(a - 1, 4 * STEPS, 4 * STEPS))
                            project(wk_s, b_s[0]).then_inc(k_done, 1)
                        if t == 2:
                            project(wq_s, b_s[1]).then_inc(q_done, 1)
                        if t == 3:
                            for s in range(GS):
                                for kt in range(KT):
                                    m = pe.matmul(b_pt[:, D * s:D * s + D], zT[:, kt, SEQ * s:SEQ * s + SEQ],
                                                  wv_s[:, kt, :], start=(kt == 0), stop=(kt == KT - 1))
                            m.then_inc(v_done, 1)
                    if f is not None:
                        if t == 3:
                            pe.wait_ge(z2_ready, at(f, GS, GS))
                            pose(z2, b_m).then_inc(z2_posed, 1)
                        if t == 4:
                            pe.wait_ge(z2T_ready, at(f, 1, 1))
                            for s in range(GS):
                                for kt in range(KT):
                                    m = pe.matmul(b_m[:, E * s:E * s + E], z2T[:, kt, SEQ * s:SEQ * s + SEQ],
                                                  rt_w[:, kt, :], start=(kt == 0), stop=(kt == KT - 1))
                            m.then_inc(l_done, 1)
                        if t == 5:
                            pe.wait_ge(route, at(f, ROUTE, ROUTE))
                            for s in range(GS):
                                m = pe.transpose(b_m[0:PARTS * E, SEQ // 2 * s:SEQ // 2 * s + SEQ // 2].bitcast(BF16),
                                                 wparts[:, s].rearrange("p c e -> p (c e)"), ident_b[:])
                            m.then_inc(w_posed, 1)
                        if 6 <= t < 6 + E // 2:
                            j = t - 6
                            if j == 0:
                                pe.wait_ge(wT_ready, at(f, 1, 1))
                            else:
                                pe.wait_ge(wbc_ready, at(f, E // 2, j))
                            for e2 in range(2):
                                m = pe.matmul(b_m[:, GT * e2:GT * e2 + GT], sel_b[:, 2 * j + e2, :], wT[:],
                                              start=True, stop=True)
                            m.then_inc(wbc_done, 1)
                    if a is not None:
                        if t == 3:
                            pe.wait_ge(v_ready, at(a, 1, 1))
                            if later(a):
                                pe.wait_ge(cu_ready, at(a - 1, GS, GS))
                                pe.wait_ge(c_ready, at(a - 1, GS * KT, GS * KT))
                            for s in range(GS):
                                for kt in range(KT):
                                    m = pe.matmul(b_ct[:, s * KT + kt:s * KT + kt + 1], v_s[:, s, P * kt:P * kt + P],
                                                  eps_col[:], start=True, stop=True)
                            m.then_inc(vs_done, 1)
                        if 4 <= t < 4 + STEPS:
                            scores(a, t - 4)
                        if 5 <= t < 5 + STEPS:
                            pose_p(a, t - 5)
                        if 6 <= t < 6 + STEPS:
                            weigh_v(a, t - 6)
                        if t in (10, 13):
                            s = (t - 10) // 3
                            pe.wait_ge(r_ready, at(a, GS, s + 1))
                            if s == 0:
                                if f is not None:
                                    pe.wait_ge(wbc_ready, at(f, E // 2, E // 2))
                            else:
                                pe.wait_ge(h1_ready, at(a, GS, s))
                            pe.transpose(b_m[0:HEADS, 0:SEQ], rsm[:, s, :], ident_f[:]).then_inc(r_posed, 1)
                        if t in (11, 14):
                            s = (t - 11) // 3
                            pe.wait_ge(rT_ready, at(a, GS, s + 1))
                            for kt in range(KT):
                                m = pe.matmul(b_m[:, SEQ * (kt + 1):SEQ * (kt + 2)], pick_f[:, kt, :], rT[:, s, :],
                                              start=True, stop=True)
                            m.then_inc(rbc_done, 1)
                    if f is not None:
                        for u in GU_SLOT.get(t, []):
                            gate_up(f, u)
                            if u >= 2:
                                down_of(f, u - 2)
                        if t == SLOTS - 1:
                            down_of(f, UNITS - 2)
                            down_of(f, UNITS - 1)
                    if a is not None and t in (12, 15):
                        s = (t - 12) // 3
                        pe.wait_ge(c_ready, at(a, GS * KT, KT * (s + 1)))
                        for kt in range(KT):
                            m = pe.matmul(b_m[:, 0:D], cx[:, s, kt, :], wo_s[:, kt, :],
                                          start=(kt == 0), stop=(kt == KT - 1))
                        m.then_inc(o_done, 1)

            bodies(step, pe)


def base_pe_table():
    pe = np.zeros((SEQ, D), dtype=np.float32)
    position = np.arange(SEQ, dtype=np.float32)[:, None]
    div_term = np.exp(np.arange(0, D, 2, dtype=np.float32) * (-np.log(10000.0) / D))
    pe[:, 0::2] = np.sin(position * div_term)
    pe[:, 1::2] = np.cos(position * div_term)
    return pe


def shape_constants():
    ident = np.eye(P, dtype=np.float32)
    mask = np.where(np.arange(P)[None, :] > np.arange(P)[:, None], MASKED, 0.0).astype(np.float32)
    pick = np.zeros((HEADS, KT, P), np.float32)
    for hd in range(HEADS):
        pick[hd, hd // HT, DK * (hd % HT):DK * (hd % HT) + DK] = 1.0
    sel = np.zeros((PARTS * E, E, P), np.float32)
    for e in range(E):
        sel[e::E, e, :] = 0.5
    return ident, mask, pick, sel


def kernel(x, L0_tok_weight, L0_tok_gamma, L0_tok_beta, L0_attn_Wq, L0_attn_bq, L0_attn_Wk, L0_attn_bk,
           L0_attn_Wv, L0_attn_bv, L0_attn_Wo, L0_attn_bo, L0_ffn_router_w, L0_ffn_w_gate, L0_ffn_w_up,
           L0_ffn_w_down, L0_ffn_ws_gate, L0_ffn_ws_up, L0_ffn_ws_down):
    import concourse.bacc as bacc
    from concourse.bass_utils import run_bass_kernel_spmd

    ident, mask, pick, sel = shape_constants()
    c = np.ascontiguousarray
    arrays = {
        "ids": c(np.asarray(x).T), "table": L0_tok_weight, "base_pe": base_pe_table(),
        "gamma": L0_tok_gamma, "beta": L0_tok_beta,
        "wq": c(np.asarray(L0_attn_Wq).T), "bq": c(np.asarray(L0_attn_bq).reshape(KT, P).T), "wk": c(np.asarray(L0_attn_Wk).T), "bk": c(np.asarray(L0_attn_bk).reshape(KT, P).T),
        "wv": c(np.asarray(L0_attn_Wv).T), "bv": L0_attn_bv, "wo": c(np.asarray(L0_attn_Wo).T), "bo": L0_attn_bo,
        "router": L0_ffn_router_w, "gate": L0_ffn_w_gate, "up": L0_ffn_w_up, "down": L0_ffn_w_down,
        "s_gate": L0_ffn_ws_gate, "s_up": L0_ffn_ws_up, "s_down": L0_ffn_ws_down,
        "ident": ident, "mask": mask, "pick": pick, "sel": sel,
    }
    nc = bacc.Bacc("TRN2", target_bir_lowering=False, num_devices=1)
    feeds, args = {}, []
    for name, a in arrays.items():
        a = c(a)
        feeds[f"in_{name}"] = a
        args.append(nc.dram_tensor(f"in_{name}", a.shape, mybir.dt.from_np(a.dtype), kind="ExternalInput").ap())
    shape = (x.shape[0], SEQ, D)
    args.append(nc.dram_tensor("out", shape, F32, kind="ExternalOutput").ap())
    build(nc, *args)
    r = run_bass_kernel_spmd(nc, [feeds], core_ids=[0])
    return r.results[0]["out"]
```

```python
from contextlib import ExitStack

import numpy as np

import concourse.bass as bass
from concourse import mybir

F32 = mybir.dt.float32
F32R = mybir.dt.float32r
BF16 = mybir.dt.bfloat16
I32 = mybir.dt.int32
ALU = mybir.AluOpType
ACT = mybir.ActivationFunctionType
AX = mybir.AxisListType
RED = bass.bass_isa.ReduceOp

P = 128
SEQ = 128
D = 256
KT = D // P
GS = 2
GT = GS * SEQ
HEADS = 16
DK = D // HEADS
QK_SCALE = 1.0 / 4.0
HT = HEADS // KT
QUADS = HEADS // 4
STEPS = GS * QUADS
E = 8
TOP_K = 6
FS = 256
UNITS = FS // P + E
SHARED = FS // P
PRS = 3
HBUF = 4
EPS = 1e-5
QMIN, QMAX = -128.0, 127.0
ROUND = 1.5 * 2.0 ** 23
MASKED = -1e30
ATTN_EPS = 1e-9
PARTS = 3

LAG = 2
FIRST = {6: [0], 7: [1], 8: [2], 9: [3], 10: [4], 11: [5]}
CARRY = {0: [6], 1: [7], 2: [8], 4: [9], 5: [10], 6: [11]}
SLOTS = 13
UNROLL = 4


def at(g, per_group, k):
    return g * per_group + k


def later(g):
    return not (isinstance(g, int) and g == 0)


def build(nc, ids, table, base_pe, gamma, beta, wq, bq, wk, bk, wv, bv, wo, bo,
          router, gate, up, down, s_gate, s_up, s_down, ident, ident16, mask, pick, sel, out):
    n_rows = table.shape[0]
    batch = ids.shape[1]
    groups = batch // GS
    cols = n_rows * D // P
    n_chunk = 58
    assert cols % n_chunk == 0 and batch % GS == 0
    chunk = cols // n_chunk
    RING = 3
    flat = table.rearrange("r d -> (r d)").rearrange("(p c) -> p c", p=P)

    def held(eng, k):
        eng.sem_inc(waits_over[k], 1)

    with ExitStack() as ctx:
        def sb(name, shape, dt=F32):
            return ctx.enter_context(nc.sbuf_tensor(name, shape, dt))

        def bank(name):
            return ctx.enter_context(nc.psum_tensor(name, [P, 512], F32))

        def sem(name):
            return ctx.enter_context(nc.semaphore(name))

        def pair(name, shape):
            return [sb(f"{name}_{part}", shape, F32R) for part in ("hi", "lo")]

        proj_w = pair("proj_w", [P, 4, KT, D])
        gu_w = pair("gu_w", [P, UNITS, 2, KT, P])
        dn_w = pair("dn_w", [P, UNITS, D])
        rt_w = pair("rt_w", [P, KT, E])
        rt_raw = sb("rt_raw", [P, KT, E])
        bq_s, bk_s = sb("bq_s", [P, KT]), sb("bk_s", [P, KT])
        bv_s, bo_s, gamma_s, beta_s = (sb(n, [P, D]) for n in ("bv_s", "bo_s", "gamma_s", "beta_s"))
        pe_s = sb("pe_s", [P, D])
        ident_f = sb("ident_f", [P, P])
        ident_b = sb("ident_b", [P, P], BF16)
        mask_b = sb("mask_b", [P, P], BF16)
        pick_r = sb("pick_r", [HEADS, KT, P], F32R)
        sel_b = sb("sel_b", [PARTS * E, E, P], BF16)
        eps_col = sb("eps_col", [P, 1])
        half_pow = sb("half_pow", [P, GS])
        ids_s = sb("ids_s", [P, batch], I32)
        lows, highs = sb("lows", [P, n_chunk]), sb("highs", [P, n_chunk])
        ext, ext_all = sb("ext", [P, 2]), sb("ext_all", [P, 2])
        span, scale, inv, wr, zp = (sb(n, [P, 1]) for n in ("span", "scale", "inv", "wr", "zp"))

        early = sb("early", [P, max(RING * chunk, 44 * P)])
        ring = early[:, 0:RING * chunk].rearrange("p (j c) -> p j c", j=RING)
        late = sb("late", [P, 4 * KT * D + UNITS * (2 * KT * P + D)])

        def views(arena):
            used = [0]

            def view(*dims):
                n = int(np.prod(dims))
                v = arena[:, used[0]:used[0] + n]
                used[0] += n
                names = "abcd"[:len(dims)]
                return v.rearrange(f"p ({' '.join(names)}) -> p {' '.join(names)}", **dict(zip(names, dims)))

            return view

        raw_view, early_view, late_view = views(late), views(early), views(late)
        proj_raw = raw_view(4, KT, D)
        gu_raw = raw_view(UNITS, 2, KT, P)
        dn_raw = raw_view(UNITS, D)
        gi = sb("gi", [P, GS], I32)
        raw, xe, xn, h, z, hb = (late_view(GS, D) for _ in range(6))
        st1, st2, st3 = (sb(n, [P, GS, 6]) for n in ("st1", "st2", "st3"))
        mv1, mv2, mv3 = (sb(n, [P, GS, 2]) for n in ("mv1", "mv2", "mv3"))
        ve1, ve2, ve3 = (sb(n, [P, GS]) for n in ("ve1", "ve2", "ve3"))
        rs1, rs2, rs3 = (sb(n, [P, GS]) for n in ("rs1", "rs2", "rs3"))
        zT, qT = pair("zT", [P, KT, GT]), pair("qT", [P, KT, GT])
        kT = early_view(2, GS, KT, SEQ)
        kbd = sb("kbd", [P, 2, GS, KT, HT, SEQ], F32R)
        v_s = late_view(GS, D)
        vpad = early_view(GS, HEADS, 2 * DK)
        vs = sb("vs", [P, GS * KT])
        nm = sb("nm", [P, STEPS, 4])
        sm, rsm = sb("sm", [P, GS, HEADS]), sb("rsm", [P, GS, HEADS])
        pr = early_view(PRS, 4, SEQ)
        pT = early_view(2, 4, SEQ)
        rT = pair("rT", [HEADS, GT])
        cu = early_view(GS, KT * SEQ)
        cx = early_view(GS, KT, SEQ)
        cxp = pair("cxp", [P, GS, KT, SEQ])
        h1, z2, res = (late_view(GS, D) for _ in range(3))
        z2T = pair("z2T", [P, KT, GT])
        lT_or_pick = sb("lT_or_pick", [HEADS, GT])
        lT, pick_raw = lT_or_pick[0:E, :], lT_or_pick[:].rearrange("p (t n) -> p t n", t=KT)
        lmax, esum, erec = sb("lmax", [P, GS]), sb("esum", [P, GS]), sb("erec", [P, GS])
        ex = sb("ex", [P, GS, E])
        p10 = sb("p10", [P, GS, E + 2])
        left = sb("left", [P, GS, E + 2])
        top = sb("top", [P, GS, 8])
        strike = sb("strike", [P, GS, 2])
        wts, wr1 = (sb(n, [P, GS, E]) for n in ("wts", "wr1"))
        wparts = sb("wparts", [P, GS, PARTS, E], BF16)
        wT = sb("wT", [PARTS * E, GT], BF16)
        wbc = late_view(E, GT)
        tn, ga, gb, hw = (late_view(2, GT) for _ in range(4))
        hh = pair("hh", [P, HBUF, GT])
        ob = late_view(GS, D)

        b_s = [bank("b_s0"), bank("b_s1")]
        b_pt = bank("b_pt")
        b_ct = bank("b_ct")
        b_m = bank("b_m")
        b_g = [bank("b_g0"), bank("b_g1")]
        b_y = bank("b_y")

        w_load = sem("w_load")
        q_scaled = sem("q_scaled")
        waits_over = [sem("pool_waits_over"), sem("dve_waits_over"), sem("pe_waits_over")]
        chunk_in = [sem(f"chunk_in{j}") for j in range(RING)]
        chunk_used, range_step, range_all = sem("chunk_used"), sem("range_step"), sem("range_all")
        consts, w_hi, w_lo, cleared = sem("consts"), sem("w_hi"), sem("w_lo"), sem("cleared")
        idx_copied, gathered = sem("idx_copied"), sem("gathered")
        quant, stats1, mean1, var1, rstd1, normed1, scaled1, h_ready = (sem(n) for n in (
            "quant", "stats1", "mean1", "var1", "rstd1", "normed1", "scaled1", "h_ready"))
        stats2, mean2, var2, rstd2, z_ready, hb_ready = (sem(n) for n in (
            "stats2", "mean2", "var2", "rstd2", "z_ready", "hb_ready"))
        z_posed, zT_hi, zT_ready, k_done, k_hi, k_ready, kbd_ready = (sem(n) for n in (
            "z_posed", "zT_hi", "zT_ready", "k_done", "k_hi", "k_ready", "kbd_ready"))
        q_done, q_hi, q_ready = (sem(n) for n in ("q_done", "q_hi", "q_ready"))
        v_done, v_ready, vpad_ready, vs_done, vs_ready = (sem(n) for n in (
            "v_done", "v_ready", "vpad_ready", "vs_done", "vs_ready"))
        s_done, max_ready, exp_done, p_posed, pT_ready, pv_done = (sem(n) for n in (
            "s_done", "max_ready", "exp_done", "p_posed", "pT_ready", "pv_done"))
        r_ready, r_posed, rT_ready, rbc_done, cu_ready, c_mul, c_hi, c_ready, o_done = (sem(n) for n in (
            "r_ready", "r_posed", "rT_ready", "rbc_done", "cu_ready", "c_mul", "c_hi", "c_ready", "o_done"))
        h1_ready, stats3, mean3, var3, rstd3, z2_ready, res_ready = (sem(n) for n in (
            "h1_ready", "stats3", "mean3", "var3", "rstd3", "z2_ready", "res_ready"))
        z2T_hi, l_raw, lT_ready = sem("z2T_hi"), sem("l_raw"), sem("lT_ready")
        h_hi, h_lo, rT_hi = sem("h_hi"), sem("h_lo"), sem("rT_hi")
        z2_posed, z2T_ready, l_done, l_max, r_exp, route = (sem(n) for n in (
            "z2_posed", "z2T_ready", "l_done", "l_max", "r_exp", "route"))
        w_posed, wT_ready, wbc_done, wbc_ready = (sem(n) for n in ("w_posed", "wT_ready", "wbc_done", "wbc_ready"))
        gu_done, tanh_done, a_done, b_done, hw_done, d_done, out_ready, out_sent = (sem(n) for n in (
            "gu_done", "tanh_done", "a_done", "b_done", "hw_done", "d_done", "out_ready", "out_sent"))

        ROUTE = 12
        KBD = 16 * HT
        W_LOADS = 16 * 28

        def bodies(step, eng):
            step(0, None, None, None)
            step(1, 0, None, None)
            step(2, 1, 0, None)
            step(3, 2, 1, 0)
            for a in range(3, 3 + (groups - 5) % UNROLL):
                step(a + 1, a, a - 1, a - 2)
            with eng.Fori(0, (groups - 5) // UNROLL) as r:
                for k in range(UNROLL):
                    a = r * UNROLL + (3 + (groups - 5) % UNROLL + k)
                    step(a + 1, a, a - 1, a - 2)
            step(groups - 1, groups - 2, groups - 3, groups - 4)
            step(None, groups - 1, groups - 2, groups - 3)
            step(None, None, groups - 1, groups - 2)
            step(None, None, None, groups - 1)

        def has_next(e):
            return e is not None and (not isinstance(e, int) or e + 1 < groups)

        def ffn_steps(t, f, c):
            if c is not None:
                for n in CARRY.get(t, []):
                    yield c, n
            if f is not None:
                for n in FIRST.get(t, []):
                    yield f, n

        block = ctx.enter_context(nc.Block())

        @block.sync
        def _(sp):
            def load_chunk(c, j):
                sp.dma_start(ring[:, j, :], flat[:, bass.ds(c * chunk, chunk)]).then_inc(chunk_in[j], 16)

            for j in range(RING):
                load_chunk(j, j)
            with sp.Fori(1, n_chunk // RING) as r:
                for j in range(RING):
                    sp.wait_ge(chunk_used, r * 2 * RING + (2 * (j + 1) - 2 * RING))
                    load_chunk(r * RING + j, j)
            for c in range(n_chunk // RING * RING, n_chunk):
                sp.wait_ge(chunk_used, 2 * (c - RING + 1))
                load_chunk(c, c % RING)

            def step(e, a, f, c):
                if c is not None:
                    sp.wait_ge(out_ready, at(c, 1, 1))
                    sp.dma_start(out[bass.ds(c * GS, GS)].rearrange("s p d -> p s d"), ob).then_inc(out_sent, 16)
                if e is not None:
                    sp.wait_ge(k_ready, at(e, KT, KT))
                    if later(e):
                        sp.wait_ge(s_done, at(e - 1, STEPS, STEPS))
                    for j in range(HT):
                        sp.dma_start(kbd[DK * j:DK * j + DK, :, :, :, j, :].bitcast(F32).rearrange("p c s t n -> p (c s t) n"),
                                     kT[DK * j:DK * j + DK].rearrange("p c s t n -> p (c s t) n")).then_inc(kbd_ready, 16)

            bodies(step, sp)
            sp.wait_ge(out_sent, 16 * groups)

        @block.gpsimd
        def _(pool):
            pool.memset(eps_col[:], ATTN_EPS).then_inc(consts, 1)
            pool.memset(half_pow[:], -0.5).then_inc(consts, 1)
            pool.memset(strike[:, :, 0:1], -1.0).then_inc(consts, 1)
            pool.memset(strike[:, :, 1:2], -2.0).then_inc(consts, 1)
            pool.memset(p10[:, :, E:E + 1], -1.0).then_inc(consts, 1)
            pool.memset(p10[:, :, E + 1:E + 2], -2.0).then_inc(consts, 1)
            pool.memset(kbd[:].bitcast(F32), 0.0).then_inc(consts, 1)
            pool.wait_ge(w_load, W_LOADS)
            pool.tensor_scalar(proj_raw[:, 0], proj_raw[:, 0], QK_SCALE, 0.0, ALU.mult, ALU.add).then_inc(q_scaled, 1)
            pool.tensor_scalar(bq_s[:], bq_s[:], QK_SCALE, 0.0, ALU.mult, ALU.add).then_inc(q_scaled, 1)

            for n, ((hi, lo), w) in enumerate(((proj_w, proj_raw), (gu_w, gu_raw), (dn_w, dn_raw), (rt_w, rt_raw[:]))):
                pool.wait_ge(w_hi, n + 1)
                pool.tensor_tensor(lo[:], w, hi[:].bitcast(F32), ALU.subtract).then_inc(w_lo, 1)

            def gather(g):
                if later(g):
                    pool.wait_ge(gathered, at(g - 1, 32, 32))
                    pool.wait_ge(quant, at(g - 1, 4, 1))
                held(pool, 0)
                pool.tensor_copy(gi[:], ids_s[:, bass.ds(g * GS, GS)]).then_inc(idx_copied, 1)
                pool.wait_ge(idx_copied, at(g, 1, 1))
                for s in range(GS):
                    held(pool, 0)
                    pool.indirect_dma_start(
                        raw[:, s, :], None, table,
                        bass.IndirectOffsetOnAxis(ap=gi[:, s:s + 1].bitcast(mybir.dt.uint32), axis=0)).then_inc(gathered, 16)

            def rstd(g, mean, k, mv, ve, rs, var, done, per, s):
                pool.wait_ge(mean, at(g, GS, k))
                held(pool, 0)
                pool.tensor_scalar(ve[:, s], mv[:, s, 1], EPS, 1.0, ALU.add, ALU.mult).then_inc(var, 1)
                pool.wait_ge(var, at(g, per, k * per // GS))
                pool.tensor_tensor(rs[:, s], ve[:, s], half_pow[:, s], ALU.pow).then_inc(done, 1)

            def scale_h(g, half):
                if half == 0:
                    pool.wait_ge(normed1, at(g, GS, GS))
                    if later(g):
                        pool.wait_ge(z_ready, at(g - 1, GS, GS))
                        pool.wait_ge(hb_ready, at(g - 1, 1, 1))
                    pool.tensor_tensor(h[:], xn[:], gamma_s[:].unsqueeze(1).broadcast_to([P, GS, D]), ALU.mult).then_inc(scaled1, 1)
                else:
                    pool.wait_ge(scaled1, at(g, 1, 1))
                    pool.tensor_tensor(h[:], h[:], beta_s[:].unsqueeze(1).broadcast_to([P, GS, D]), ALU.add).then_inc(h_ready, 1)

            def residual(g):
                pool.wait_ge(h_ready, at(g, 1, 1))
                if later(g):
                    pool.wait_ge(h1_ready, at(g - 1, 1, 1))
                pool.tensor_tensor(hb[:], h[:], bo_s[:].unsqueeze(1).broadcast_to([P, GS, D]), ALU.add).then_inc(hb_ready, 1)

            def weigh(f, u):
                e = u - SHARED
                pool.wait_ge(b_done, at(f, UNITS, u + 1))
                pool.wait_ge(wbc_ready, at(f, E // 2, e // 2 + 1))
                pool.wait_ge(h_lo, at(f, UNITS, u - 1))
                pool.tensor_tensor(hw[:, u % 2, :], gb[:, u % 2, :], wbc[:, e, :], ALU.mult).then_inc(hw_done, 1)

            def low_part(f, u):
                pool.wait_ge(h_hi, at(f, UNITS, u + 1))
                pool.tensor_tensor(hh[1][:, u % HBUF, :], hw[:, u % 2, :], hh[0][:, u % HBUF, :].bitcast(F32),
                                   ALU.subtract).then_inc(h_lo, 1)

            def step(e, a, f, c):
                for t in range(SLOTS):
                    for g, n in ffn_steps(t, f, c):
                        if 1 <= n <= UNITS:
                            low_part(g, n - 1)
                        if SHARED <= n < UNITS:
                            weigh(g, n)
                    if t == 1 and has_next(e):
                        gather(e + 1)
                    if f is not None and t == 3:
                        rstd(f, mean3, GS, mv3, ve3, rs3, var3, rstd3, 1, slice(0, GS))
                    if a is not None and t == 3:
                        residual(a)
                    if e is not None:
                        if t in (4, 5):
                            scale_h(e, t - 4)
                        if t == 6:
                            rstd(e, mean2, GS, mv2, ve2, rs2, var2, rstd2, 1, slice(0, GS))
                    if t == 11 and has_next(e):
                        rstd(e + 1, mean1, GS, mv1, ve1, rs1, var1, rstd1, 1, slice(0, GS))

            pool.wait_ge(range_step, 3)
            pool.partition_all_reduce(ext_all[:], ext[:], P, RED.max).then_inc(range_all, 1)
            pool.memset(vpad, 0.0).then_inc(cleared, 1)
            pool.wait_ge(w_lo, 4)
            pool.wait_ge(w_hi, 4)
            pool.wait_ge(cleared, 1)
            gather(0)
            rstd(0, mean1, GS, mv1, ve1, rs1, var1, rstd1, 1, slice(0, GS))
            bodies(step, pool)

        @block.scalar
        def _(act):
            def load(dst, src, s=w_load):
                act.dma_start(dst, src).then_inc(s, 16)

            for k, src in enumerate((wq, wk, wv, wo)):
                load(proj_raw[:, k], src.rearrange("(t p) n -> p t n", p=P))
            load(rt_raw[:], router.rearrange("(t p) n -> p t n", p=P))
            for dst, src in ((bq_s, bq), (bk_s, bk)):
                load(dst[:], src)
            for dst, src in ((bv_s, bv), (bo_s, bo), (gamma_s, gamma), (beta_s, beta)):
                load(dst[:], src.partition_broadcast(P))
            load(pe_s[:], base_pe)
            load(ident_f[:], ident)
            load(mask_b[:], mask)
            load(pick_raw, pick)
            load(sel_b[:], sel)
            load(ident_b[:], ident16)
            load(ids_s[:], ids)
            load(dn_raw[:, 0:SHARED, :], s_down.rearrange("(u p) d -> p u d", p=P))
            load(dn_raw[:, SHARED:UNITS, :], down.rearrange("e p d -> p e d"))
            for k, (ex_w, sh_w) in enumerate(((gate, s_gate), (up, s_up))):
                for t in range(KT):
                    load(gu_raw[:, 0:SHARED, k, t, :], sh_w.rearrange("(t p) (u f) -> t p u f", p=P, f=P)[t])
                    load(gu_raw[:, SHARED:UNITS, k, t, :], ex_w.rearrange("e (t p) f -> t p e f", p=P)[t])
            act.wait_ge(w_load, W_LOADS)
            act.wait_ge(q_scaled, 2)
            for hi, w in ((proj_w[0], proj_raw), (gu_w[0], gu_raw), (dn_w[0], dn_raw), (rt_w[0], rt_raw[:])):
                act.activation(hi[:], w, ACT.Copy).then_inc(w_hi, 1)

            act.activation(pick_r[:], pick_raw, ACT.Copy).then_inc(w_hi, 1)

            def exps(a, q):
                act.wait_ge(max_ready, at(a, STEPS, q + 1))
                if q >= PRS:
                    act.wait_ge(p_posed, at(a, STEPS, q - PRS + 1))
                elif later(a):
                    act.wait_ge(p_posed, at(a - 1, STEPS, STEPS))
                s, c = divmod(q, QUADS)
                for j in range(4):
                    hd = 4 * c + j
                    act.activation(pr[:, q % PRS, j, :], b_s[q % 2][:, SEQ * j:SEQ * j + SEQ], ACT.Exp,
                                   bias=nm[:, q, j:j + 1], accum_out=sm[:, s, hd:hd + 1]).then_inc(exp_done, 1)

            def high_part(f, u):
                if u < SHARED:
                    act.wait_ge(b_done, at(f, UNITS, u + 1))
                else:
                    act.wait_ge(hw_done, at(f, E, u - SHARED + 1))
                if u >= HBUF:
                    act.wait_ge(d_done, at(f, UNITS, u - HBUF + 1))
                elif later(f):
                    act.wait_ge(d_done, at(f - 1, UNITS, u - HBUF + UNITS + 1))
                act.activation(hh[0][:, u % HBUF, :], hw[:, u % 2, :], ACT.Copy).then_inc(h_hi, 1)

            def step(e, a, f, c):
                for t in range(SLOTS):
                    if f is not None and t == 2:
                        act.wait_ge(c_mul, at(f, 1, 1))
                        for s in range(GS):
                            for kt in range(KT):
                                act.activation(cxp[0][:, s, kt], cx[:, s, kt], ACT.Identity,
                                               bias=vs[:, s * KT + kt:s * KT + kt + 1]).then_inc(c_hi, 1)
                    if f is not None and t == 7:
                        act.wait_ge(l_max, at(f, 1, 1))
                        for s in range(GS):
                            act.activation(ex[:, s, :], b_m[:, GT + E * s:GT + E * s + E], ACT.Exp,
                                           bias=lmax[:, s:s + 1], accum_out=esum[:, s:s + 1]).then_inc(r_exp, 1)
                    if f is not None and t == 0:
                        act.wait_ge(r_posed, at(f, 1, 1))
                        act.activation(rT[0][:], b_m[0:HEADS, 0:GT], ACT.Copy).then_inc(rT_hi, 1)
                    if f is not None and t == 5:
                        act.wait_ge(z2_posed, at(f, 1, 1))
                        if later(f):
                            act.wait_ge(gu_done, at(f - 1, UNITS, UNITS))
                        act.activation(z2T[0][:].rearrange("p t n -> p (t n)"), b_m[:], ACT.Copy).then_inc(z2T_hi, 1)
                    if a is not None and t < STEPS:
                        exps(a, t)
                    if f is not None:
                        if t == 6:
                            act.wait_ge(l_raw, at(f, 1, 1))
                            act.activation(lT, b_m[0:E, 0:GT], ACT.Copy).then_inc(lT_ready, 1)
                    if e is not None:
                        if t == 8:
                            act.wait_ge(z_posed, at(e, 1, 1))
                            if later(e):
                                act.wait_ge(v_done, at(e - 1, 1, 1))
                            act.activation(zT[0][:].rearrange("p t n -> p (t n)"), b_s[0][:], ACT.Copy).then_inc(zT_hi, 1)
                        if t == 9:
                            act.wait_ge(k_done, at(e, 1, 1))
                            if later(e):
                                act.wait_ge(kbd_ready, at(e - 1, KBD, KBD))
                            for kt in range(KT):
                                act.activation(kT[:, 0, :, kt, :].bitcast(F32R),
                                               b_s[1][:, GT * kt:GT * kt + GT].rearrange("p (s n) -> p s n", s=GS),
                                               ACT.Identity, bias=bk_s[:, kt:kt + 1]).then_inc(k_hi, 1)
                    if f is not None and t == 9:
                        act.wait_ge(w_posed, at(f, 1, 1))
                        act.activation(wT[:], b_m[0:PARTS * E, 0:GT // 2].bitcast(BF16), ACT.Copy).then_inc(wT_ready, 1)
                    if a is not None and t == 10:
                        act.wait_ge(pv_done, at(a, STEPS, STEPS))
                        if later(a):
                            act.wait_ge(c_mul, at(a - 1, 1, 1))
                        act.activation(cu.rearrange("p s n -> p (s n)"), b_ct[:], ACT.Copy).then_inc(cu_ready, 1)
                    if e is not None:
                        if t == 10:
                            act.wait_ge(q_done, at(e, 1, 1))
                            for kt in range(KT):
                                act.activation(qT[0][:, kt, :], b_s[0][:, GT * kt:GT * kt + GT], ACT.Identity,
                                               bias=bq_s[:, kt:kt + 1]).then_inc(q_hi, 1)
                    if f is not None and 9 <= t < 9 + E // 2:
                        j = t - 9
                        act.wait_ge(wbc_done, at(f, E // 2, j + 1))
                        if later(f):
                            act.wait_ge(hw_done, at(f - 1, E, 2 * j + 2))
                        act.activation(wbc[:, 2 * j:2 * j + 2, :].rearrange("p e n -> p (e n)"), b_m[:],
                                       ACT.Copy).then_inc(wbc_ready, 1)
                    for g, n in ffn_steps(t, f, c):
                        if 1 <= n <= UNITS:
                            high_part(g, n - 1)
                        if n < UNITS:
                            act.wait_ge(gu_done, at(g, UNITS, n + 1))
                            act.activation(tn[:, n % 2, :], b_g[n % 2][:, 0:GT], ACT.Tanh, scale=0.5).then_inc(tanh_done, 1)
                    if f is not None and t == 10:
                        if later(f):
                            act.wait_ge(out_ready, at(f - 1, 1, 1))
                        act.wait_ge(h1_ready, at(f, 1, 1))
                        act.activation(res[:], h1[:], ACT.Copy).then_inc(res_ready, 1)
                    if e is not None and t == 12:
                        act.wait_ge(v_ready, at(e, 1, 1))
                        if later(e):
                            act.wait_ge(pv_done, at(e - 1, STEPS, STEPS))
                        for o in range(2):
                            act.activation(vpad.rearrange("p s (j o) c -> p s j o c", o=2)[:, :, :, o, DK * o:DK * o + DK],
                                           v_s.rearrange("p s (j o d) -> p s j o d", o=2, d=DK)[:, :, :, o, :],
                                           ACT.Copy).then_inc(vpad_ready, 1)

            bodies(step, act)

        @block.vector
        def _(dve):
            def extremes(c, j, seen):
                dve.wait_ge(chunk_in[j], seen)
                dve.tensor_reduce(highs[:, bass.ds(c, 1)], ring[:, j, :], AX.X, ALU.max).then_inc(chunk_used, 1)
                dve.tensor_reduce(lows[:, bass.ds(c, 1)], ring[:, j, :], AX.X, ALU.min).then_inc(chunk_used, 1)

            with dve.Fori(0, n_chunk // RING) as r:
                for j in range(RING):
                    extremes(r * RING + j, j, r * 16 + 16)
            for c in range(n_chunk // RING * RING, n_chunk):
                extremes(c, c % RING, 16 * (c // RING + 1))
            dve.wait_ge(chunk_used, 2 * n_chunk)
            dve.tensor_reduce(ext[:, 0:1], highs[:], AX.X, ALU.max).then_inc(range_step, 1)
            dve.tensor_reduce(ext[:, 1:2], lows[:], AX.X, ALU.min).then_inc(range_step, 1)
            dve.wait_ge(range_step, 2)
            dve.tensor_scalar(ext[:, 1:2], ext[:, 1:2], -1.0, None, ALU.mult).then_inc(range_step, 1)
            dve.wait_ge(range_all, 1)
            dve.tensor_tensor(span[:], ext_all[:, 0:1], ext_all[:, 1:2], ALU.add).then_inc(range_step, 1)
            dve.wait_ge(range_step, 4)
            dve.tensor_scalar(scale[:], span[:], 1.0 / (QMAX - QMIN), None, ALU.mult).then_inc(range_step, 1)
            dve.wait_ge(range_step, 5)
            dve.reciprocal(inv[:], scale[:]).then_inc(range_step, 1)
            dve.wait_ge(range_step, 6)
            dve.tensor_tensor(wr[:], ext_all[:, 1:2], inv[:], ALU.mult).then_inc(range_step, 1)
            dve.wait_ge(range_step, 7)
            dve.tensor_scalar(zp[:], wr[:], QMIN, None, ALU.add).then_inc(range_step, 1)
            dve.wait_ge(range_step, 8)
            dve.wait_ge(consts, 7)
            dve.wait_ge(cleared, 1)

            def quantise(g, part):
                if part == 0:
                    dve.wait_ge(gathered, at(g, 32, 32))
                    if later(g):
                        dve.wait_ge(normed1, at(g - 1, GS, GS))
                    dve.tensor_scalar(xe[:], raw[:], inv[:], zp[:], ALU.mult, ALU.add).then_inc(quant, 1)
                    dve.wait_ge(quant, at(g, 4, 1))
                    dve.tensor_scalar(xe[:], xe[:], QMAX, QMIN, ALU.min, ALU.max).then_inc(quant, 1)
                if part == 1:
                    dve.wait_ge(quant, at(g, 4, 2))
                    dve.tensor_scalar(xe[:], xe[:], ROUND, ROUND, ALU.add, ALU.subtract).then_inc(quant, 1)
                    dve.wait_ge(quant, at(g, 4, 3))
                    dve.tensor_scalar(xe[:], xe[:], zp[:], scale[:], ALU.subtract, ALU.mult).then_inc(quant, 1)
                if part == 2:
                    dve.wait_ge(quant, at(g, 4, 4))
                    dve.tensor_tensor(xe[:], xe[:], pe_s[:].unsqueeze(1).broadcast_to([P, GS, D]), ALU.add).then_inc(stats1, 1)
                    dve.wait_ge(stats1, at(g, 1 + GS, 1))
                    for s in range(GS):
                        dve.bn_stats(st1[:, s, :], xe[:, s, :]).then_inc(stats1, 1)
                    for s in range(GS):
                        dve.wait_ge(stats1, at(g, 1 + GS, s + 2))
                        held(dve, 1)
                        dve.bn_aggr(mv1[:, s, :], st1[:, s, :]).then_inc(mean1, 1)

            def normalise(g, x, mv, rs, y, rstd, k, per, s, done):
                dve.wait_ge(rstd, at(g, per, k))
                dve.tensor_scalar(y[:, s, :], x[:, s, :], mv[:, s, 0:1], rs[:, s:s + 1], ALU.subtract, ALU.mult).then_inc(done, 1)

            def norm1(g):
                if later(g):
                    dve.wait_ge(scaled1, at(g - 1, 1, 1))
                for s in range(GS):
                    normalise(g, xe, mv1, rs1, xn, rstd1, 1, 1, s, normed1)

            def stat2(g):
                dve.wait_ge(h_ready, at(g, 1, 1))
                for s in range(GS):
                    dve.bn_stats(st2[:, s, :], h[:, s, :]).then_inc(stats2, 1)
                for s in range(GS):
                    dve.wait_ge(stats2, at(g, GS, s + 1))
                    held(dve, 1)
                    dve.bn_aggr(mv2[:, s, :], st2[:, s, :]).then_inc(mean2, 1)

            def norm2(g):
                if later(g):
                    dve.wait_ge(z_posed, at(g - 1, 1, 1))
                for s in range(GS):
                    normalise(g, h, mv2, rs2, z, rstd2, 1, 1, s, z_ready)

            def max_of(a, q):
                dve.wait_ge(s_done, at(a, STEPS, q + 1))
                dve.tensor_reduce(nm[:, q, :], b_s[q % 2][:].rearrange("p (j n) -> p j n", j=4), AX.X, ALU.max,
                                  negate=True).then_inc(max_ready, 1)

            def keep_pT(a, q):
                dve.wait_ge(p_posed, at(a, STEPS, q + 1))
                if q >= 2:
                    dve.wait_ge(pv_done, at(a, STEPS, q - 1))
                elif later(a):
                    dve.wait_ge(pv_done, at(a - 1, STEPS, STEPS + q - 1))
                dve.tensor_copy(pT[:, q % 2].rearrange("p j n -> p (j n)"), b_pt[:]).then_inc(pT_ready, 1)

            def route_softmax(f):
                dve.wait_ge(r_exp, at(f, GS, GS))
                dve.reciprocal(erec[:], esum[:]).then_inc(route, 1)
                dve.wait_ge(route, at(f, ROUTE, 1))
                dve.tensor_tensor(p10[:, :, 0:E], ex[:], erec[:].unsqueeze(2).broadcast_to([P, GS, E]),
                                  ALU.mult).then_inc(route, 1)

            def route_choose(f):
                dve.wait_ge(route, at(f, ROUTE, 2))
                for s in range(GS):
                    held(dve, 1)
                    dve.max(top[:, s, :], p10[:, s, 0:E]).then_inc(route, 1)
                dve.wait_ge(route, at(f, ROUTE, 4))
                dve.tensor_copy(top[:, :, TOP_K:8], strike[:]).then_inc(route, 1)
                dve.wait_ge(route, at(f, ROUTE, 5))
                for s in range(GS):
                    held(dve, 1)
                    dve.match_replace(left[:, s, :], top[:, s, :], p10[:, s, :], 0.0).then_inc(route, 1)
                dve.wait_ge(route, at(f, ROUTE, 7))
                dve.tensor_tensor(wts[:], p10[:, :, 0:E], left[:, :, 0:E], ALU.subtract).then_inc(route, 1)
                dve.wait_ge(route, at(f, ROUTE, 8))
                dve.tensor_copy(wparts[:, :, 0, :], wts[:]).then_inc(route, 1)
                dve.wait_ge(route, at(f, ROUTE, 9))
                dve.tensor_tensor(wr1[:], wts[:], wparts[:, :, 0, :], ALU.subtract).then_inc(route, 1)
                dve.tensor_tensor(wparts[:, :, 1, :], wts[:], wparts[:, :, 0, :], ALU.subtract).then_inc(route, 1)
                dve.wait_ge(route, at(f, ROUTE, 11))
                dve.tensor_tensor(wparts[:, :, 2, :], wr1[:], wparts[:, :, 1, :], ALU.subtract).then_inc(route, 1)

            def gated(f, u):
                dve.wait_ge(tanh_done, at(f, UNITS, u + 1))
                dve.scalar_tensor_tensor(ga[:, u % 2, :], tn[:, u % 2, :], 1.0, b_g[u % 2][:, 0:GT],
                                         ALU.add, ALU.mult).then_inc(a_done, 1)
                dve.wait_ge(a_done, at(f, UNITS, u + 1))
                if u < SHARED:
                    if later(f):
                        dve.wait_ge(h_lo, at(f - 1, UNITS, UNITS - 1 + u))
                    dve.scalar_tensor_tensor(hw[:, u, :], ga[:, u % 2, :], 0.5, b_g[u % 2][:, GT:2 * GT],
                                             ALU.mult, ALU.mult).then_inc(b_done, 1)
                else:
                    e = u - SHARED
                    if e >= 2:
                        dve.wait_ge(hw_done, at(f, E, e - 1))
                    elif later(f):
                        dve.wait_ge(hw_done, at(f - 1, E, E + e - 1))
                    dve.tensor_tensor(gb[:, u % 2, :], ga[:, u % 2, :], b_g[u % 2][:, GT:2 * GT], ALU.mult).then_inc(b_done, 1)

            def after_out(a):
                dve.wait_ge(o_done, at(a, 1, 1))
                dve.wait_ge(hb_ready, at(a, 1, 1))
                if later(a):
                    dve.wait_ge(res_ready, at(a - 1, 1, 1))
                dve.tensor_tensor(h1.rearrange("p s d -> p (s d)"), b_m[:], hb.rearrange("p s d -> p (s d)"),
                                  ALU.add).then_inc(h1_ready, 1)
                dve.wait_ge(h1_ready, at(a, 1, 1))
                for s in range(GS):
                    dve.bn_stats(st3[:, s, :], h1[:, s, :]).then_inc(stats3, 1)
                for s in range(GS):
                    dve.wait_ge(stats3, at(a, GS, s + 1))
                    held(dve, 1)
                    dve.bn_aggr(mv3[:, s, :], st3[:, s, :]).then_inc(mean3, 1)

            def norm3(a):
                if later(a):
                    dve.wait_ge(z2_posed, at(a - 1, 1, 1))
                for s in range(GS):
                    normalise(a, h1, mv3, rs3, z2, rstd3, 1, 1, s, z2_ready)

            def step(e, a, f, c):
                for t in range(SLOTS):
                    if f is not None and t == 7:
                        dve.wait_ge(l_done, at(f, 1, 1))
                        dve.tensor_reduce(lmax[:], b_m[:, GT:GT + GS * E].rearrange("p (s e) -> p s e", s=GS),
                                          AX.X, ALU.max, negate=True).then_inc(l_max, 1)
                    if a is not None and t < STEPS:
                        max_of(a, t)
                    if e is not None and t == 7:
                        norm2(e)
                    if e is not None and t == 9:
                        for kt in range(KT):
                            dve.wait_ge(k_hi, at(e, KT, KT))
                            dve.scalar_tensor_tensor(kT[:, 1, :, kt, :].bitcast(F32R),
                                                     b_s[1][:, GT * kt:GT * kt + GT].rearrange("p (s n) -> p s n", s=GS),
                                                     bk_s[:, kt:kt + 1], kT[:, 0, :, kt, :],
                                                     ALU.add, ALU.subtract).then_inc(k_ready, 1)
                    if a is not None and 2 <= t < 2 + STEPS:
                        keep_pT(a, t - 2)
                    if f is not None and t == 5:
                        dve.wait_ge(z2T_hi, at(f, 1, 1))
                        dve.tensor_tensor(z2T[1][:].rearrange("p t n -> p (t n)"), b_m[:],
                                          z2T[0][:].rearrange("p t n -> p (t n)").bitcast(F32),
                                          ALU.subtract).then_inc(z2T_ready, 1)
                    if f is not None and t == 2:
                        for s in range(GS):
                            for kt in range(KT):
                                dve.wait_ge(c_hi, at(f, GS * KT, s * KT + kt + 1))
                                dve.scalar_tensor_tensor(
                                    cxp[1][:, s, kt], cx[:, s, kt], vs[:, s * KT + kt:s * KT + kt + 1],
                                    cxp[0][:, s, kt].bitcast(F32), ALU.add, ALU.subtract).then_inc(c_ready, 1)
                    if e is not None and t == 8:
                        dve.wait_ge(zT_hi, at(e, 1, 1))
                        dve.tensor_tensor(zT[1][:].rearrange("p t n -> p (t n)"), b_s[0][:],
                                          zT[0][:].rearrange("p t n -> p (t n)").bitcast(F32),
                                          ALU.subtract).then_inc(zT_ready, 1)
                    if a is not None and t == 8:
                        dve.wait_ge(exp_done, at(a, 4 * STEPS, 4 * STEPS))
                        dve.reciprocal(rsm[:], sm[:]).then_inc(r_ready, 1)
                    if f is not None:
                        if t == 1:
                            dve.wait_ge(cu_ready, at(f, 1, 1))
                            dve.wait_ge(rbc_done, at(f, 1, 1))
                            dve.tensor_tensor(cx.rearrange("p s t n -> p t s n"),
                                              cu.rearrange("p s (t n) -> p t s n", t=KT),
                                              b_m[:].rearrange("p (t s n) -> p t s n", t=KT, s=GS),
                                              ALU.mult).then_inc(c_mul, 1)
                        if t == 3:
                            after_out(f)
                        if t == 4:
                            norm3(f)
                        if t == 8:
                            route_softmax(f)
                    if e is not None:
                        if t == 6:
                            stat2(e)
                        if t == 10:
                            for kt in range(KT):
                                dve.wait_ge(q_hi, at(e, KT, KT))
                                dve.scalar_tensor_tensor(qT[1][:, kt, :], b_s[0][:, GT * kt:GT * kt + GT],
                                                         bq_s[:, kt:kt + 1], qT[0][:, kt, :].bitcast(F32),
                                                         ALU.add, ALU.subtract).then_inc(q_ready, 1)
                    if f is not None and t == 8:
                        route_choose(f)
                    if a is not None and t == 11:
                        dve.wait_ge(vs_done, at(a, 1, 1))
                        if later(a):
                            dve.wait_ge(c_hi, at(a - 1, GS * KT, GS * KT))
                        dve.tensor_copy(vs[:], b_ct[:, 0:GS * KT]).then_inc(vs_ready, 1)
                    if e is not None and t == 11:
                        dve.wait_ge(v_done, at(e, 1, 1))
                        if later(e):
                            dve.wait_ge(vpad_ready, at(e - 1, 2, 2))
                            dve.wait_ge(vs_done, at(e - 1, 1, 1))
                        dve.tensor_tensor(v_s, b_pt[:].rearrange("p (s d) -> p s d", s=GS),
                                          bv_s[:].unsqueeze(1).broadcast_to([P, GS, D]), ALU.add).then_inc(v_ready, 1)
                    if c is not None and t == 7:
                        dve.wait_ge(d_done, at(c, UNITS, UNITS))
                        dve.wait_ge(res_ready, at(c, 1, 1))
                        if later(c):
                            dve.wait_ge(out_sent, at(c - 1, 16, 16))
                        dve.tensor_tensor(ob.rearrange("p s d -> p (s d)"), b_y[:], res.rearrange("p s d -> p (s d)"),
                                          ALU.add).then_inc(out_ready, 1)
                    if f is not None and t == 0:
                        dve.wait_ge(rT_hi, at(f, 1, 1))
                        dve.tensor_tensor(rT[1][:], b_m[0:HEADS, 0:GT], rT[0][:].bitcast(F32),
                                          ALU.subtract).then_inc(rT_ready, 1)
                    if e is not None and t == 0:
                        norm1(e)
                    if has_next(e) and t == 11:
                        quantise(e + 1, 2)
                    for g, n in ffn_steps(t, f, c):
                        if n < UNITS:
                            gated(g, n)
                    if has_next(e) and 9 <= t < 11:
                        quantise(e + 1, t - 9)

            for part in range(3):
                quantise(0, part)
            bodies(step, dve)

        @block.tensor
        def _(pe):
            pe.wait_ge(w_load, W_LOADS)
            pe.wait_ge(w_hi, 5)
            pe.wait_ge(w_lo, 4)
            pe.wait_ge(consts, 7)

            def pose(x, dst):
                for kt in range(KT):
                    for s in range(GS):
                        m = pe.transpose(dst[:, GT * kt + SEQ * s:GT * kt + SEQ * s + SEQ],
                                         x[:, s, P * kt:P * kt + P], ident_f[:])
                return m

            def passes(dst, lhs, rhs, start=True, stop=True, **kw):
                pe.matmul(dst, lhs[0], rhs[0], start=start, stop=False, **kw)
                pe.matmul(dst, lhs[0], rhs[1], start=False, stop=False, **kw)
                return pe.matmul(dst, lhs[1], rhs[0], start=False, stop=stop, **kw)

            def project(k, dst):
                for m in range(KT):
                    for kt in range(KT):
                        mm = passes(dst[:, GT * m:GT * m + GT], [w[:, k, kt, P * m:P * m + P] for w in proj_w],
                                    [x[:, kt, :] for x in zT], start=(kt == 0), stop=(kt == KT - 1))
                return mm

            def scores(a, q):
                s, c = divmod(q, QUADS)
                if q == 0:
                    pe.wait_ge(q_ready, at(a, KT, KT))
                    pe.wait_ge(kbd_ready, at(a, KBD, KBD))
                if q >= 2:
                    pe.wait_ge(exp_done, at(a, 4 * STEPS, 4 * (q - 1)))
                pe.matmul(b_s[q % 2][:], ident_b[:], mask_b[:].unsqueeze(1).broadcast_to([P, 4, P]), start=True, stop=False)
                t, heads = c // 2, slice(c % 2 * 4, c % 2 * 4 + 4)
                m = passes(b_s[q % 2][:], [x[:, t, SEQ * s:SEQ * s + SEQ] for x in qT],
                           [kbd[:, part, s, t, heads, :].rearrange("p j n -> p (j n)") for part in range(2)], start=False)
                m.then_inc(s_done, 1)

            def pose_p(a, q):
                pe.wait_ge(exp_done, at(a, 4 * STEPS, 4 * (q + 1)))
                if q == 0:
                    pe.wait_ge(v_ready, at(a, 1, 1))
                else:
                    pe.wait_ge(pT_ready, at(a, STEPS, q))
                for j in range(4):
                    m = pe.transpose(b_pt[:, SEQ * j:SEQ * j + SEQ], pr[:, q % PRS, j, :], ident_f[:])
                m.then_inc(p_posed, 1)

            def weigh_v(a, q):
                s, c = divmod(q, QUADS)
                t = c // 2
                pe.wait_ge(pT_ready, at(a, STEPS, q + 1))
                if q == 0:
                    pe.wait_ge(vpad_ready, at(a, 2, 2))
                    if later(a):
                        pe.wait_ge(vs_ready, at(a - 1, 1, 1))
                for j in (0, 2, 1, 3):
                    hd = 4 * c + j
                    r = hd % HT // 2 * 2 * DK
                    m = pe.matmul(b_ct[r:r + 2 * DK, D * s + SEQ * t:D * s + SEQ * t + SEQ], vpad[:, s, hd, :],
                                  pT[:, q % 2, j, :], start=(j % 2 == 0), stop=(j % 2 == 1))
                m.then_inc(pv_done, 1)

            def gate_up(f, u):
                if u == 0:
                    pe.wait_ge(z2T_ready, at(f, 1, 1))
                if u >= 2:
                    pe.wait_ge(b_done, at(f, UNITS, u - 1))
                elif later(f):
                    pe.wait_ge(b_done, at(f - 1, UNITS, UNITS + u - 1))
                for k in range(2):
                    for kt in range(KT):
                        m = passes(b_g[u % 2][:, GT * k:GT * k + GT], [w[:, u, k, kt, :] for w in gu_w],
                                   [x[:, kt, :] for x in z2T], start=(kt == 0), stop=(kt == KT - 1))
                m.then_inc(gu_done, 1)

            def down_of(f, u):
                pe.wait_ge(h_lo, at(f, UNITS, u + 1))
                if u == 0 and later(f):
                    pe.wait_ge(out_ready, at(f - 1, 1, 1))
                for s in range(GS):
                    m = passes(b_y[:, D * s:D * s + D], [x[:, u % HBUF, SEQ * s:SEQ * s + SEQ] for x in hh],
                               [w[:, u, :] for w in dn_w], start=(u == 0 and s == 0), stop=(u == UNITS - 1),
                               skip_group_check=True)
                m.then_inc(d_done, 1)

            def step(e, a, f, c):
                for t in range(SLOTS):
                    if f is not None and t == 7:
                        pe.wait_ge(lT_ready, at(f, 1, 1))
                        held(pe, 2)
                        for s in range(GS):
                            m = pe.transpose(b_m[:, GT + E * s:GT + E * s + E], lT[:, SEQ * s:SEQ * s + SEQ],
                                             ident_f[0:E, 0:E])
                        m.then_inc(l_done, 1)
                    if e is not None and t == 8:
                        pe.wait_ge(z_ready, at(e, GS, GS))
                        if later(e):
                            pe.wait_ge(exp_done, at(e - 1, 4 * STEPS, 4 * (STEPS - 1)))
                        pose(z, b_s[0]).then_inc(z_posed, 1)
                    if a is not None and t < STEPS:
                        scores(a, t)
                    if f is not None and t == 0:
                        pe.wait_ge(r_ready, at(f, 1, 1))
                        if later(f):
                            pe.wait_ge(wbc_ready, at(f - 1, E // 2, E // 2))
                        for s in range(GS):
                            m = pe.transpose(b_m[0:HEADS, SEQ * s:SEQ * s + SEQ], rsm[:, s, :], ident_f[:])
                        m.then_inc(r_posed, 1)
                    if a is not None and 2 <= t < 2 + STEPS:
                        pose_p(a, t - 2)
                    if a is not None and 3 <= t < 3 + STEPS and t != 9:
                        weigh_v(a, t - 3)
                    if f is not None:
                        if t == 1:
                            pe.wait_ge(rT_ready, at(f, 1, 1))
                            for kt in range(KT):
                                for part in range(2):
                                    m = pe.matmul(b_m[:, GT * kt:GT * kt + GT], pick_r[:, kt, :], rT[part][:],
                                                  start=(part == 0), stop=(part == 1))
                            m.then_inc(rbc_done, 1)
                        if t == 3:
                            pe.wait_ge(c_ready, at(f, GS * KT, GS * KT))
                            for s in range(GS):
                                for kt in range(KT):
                                    m = passes(b_m[:, D * s:D * s + D], [x[:, s, kt, :] for x in cxp],
                                               [w[:, 3, kt, :] for w in proj_w], start=(kt == 0), stop=(kt == KT - 1))
                            m.then_inc(o_done, 1)
                        if t == 5:
                            pe.wait_ge(z2_ready, at(f, GS, GS))
                            pose(z2, b_m).then_inc(z2_posed, 1)
                        if t == 6:
                            pe.wait_ge(z2T_ready, at(f, 1, 1))
                            for kt in range(KT):
                                m = passes(b_m[0:E, 0:GT], [w[:, kt, :] for w in rt_w], [x[:, kt, :] for x in z2T],
                                           start=(kt == 0), stop=(kt == KT - 1))
                            m.then_inc(l_raw, 1)
                    if e is not None:
                        if t == 9:
                            pe.wait_ge(zT_ready, at(e, 1, 1))
                            if later(e):
                                pe.wait_ge(exp_done, at(e - 1, 4 * STEPS, 4 * STEPS))
                            project(1, b_s[1]).then_inc(k_done, 1)
                    if e is not None and t == 11:
                        if later(e):
                            pe.wait_ge(pT_ready, at(e - 1, STEPS, STEPS))
                        for s in range(GS):
                            for kt in range(KT):
                                m = passes(b_pt[:, D * s:D * s + D], [x[:, kt, SEQ * s:SEQ * s + SEQ] for x in zT],
                                           [w[:, 2, kt, :] for w in proj_w], start=(kt == 0), stop=(kt == KT - 1))
                        m.then_inc(v_done, 1)
                    if a is not None and t == 11:
                        pe.wait_ge(cu_ready, at(a, 1, 1))
                        for s in range(GS):
                            for kt in range(KT):
                                m = pe.matmul(b_ct[:, s * KT + kt:s * KT + kt + 1], v_s[:, s, P * kt:P * kt + P],
                                              eps_col[:], start=True, stop=True)
                        m.then_inc(vs_done, 1)
                    if e is not None and t == 9:
                        project(0, b_s[0]).then_inc(q_done, 1)
                    if f is not None and t == 9:
                        pe.wait_ge(route, at(f, ROUTE, ROUTE))
                        for s in range(GS):
                            m = pe.transpose(b_m[0:PARTS * E, SEQ // 2 * s:SEQ // 2 * s + SEQ // 2].bitcast(BF16),
                                             wparts[:, s].rearrange("p c e -> p (c e)"), ident_b[:])
                        m.then_inc(w_posed, 1)
                    if a is not None and t == 9:
                        weigh_v(a, t - 3)
                    if f is not None and 9 <= t < 9 + E // 2:
                        j = t - 9
                        if j == 0:
                            pe.wait_ge(wT_ready, at(f, 1, 1))
                        else:
                            pe.wait_ge(wbc_ready, at(f, E // 2, j))
                        for e2 in range(2):
                            m = pe.matmul(b_m[:, GT * e2:GT * e2 + GT], sel_b[:, 2 * j + e2, :], wT[:],
                                          start=True, stop=True)
                        m.then_inc(wbc_done, 1)
                    for g, n in ffn_steps(t, f, c):
                        if n < UNITS:
                            gate_up(g, n)
                        if n >= LAG:
                            down_of(g, n - LAG)

            bodies(step, pe)


def base_pe_table():
    pe = np.zeros((SEQ, D), dtype=np.float32)
    position = np.arange(SEQ, dtype=np.float32)[:, None]
    div_term = np.exp(np.arange(0, D, 2, dtype=np.float32) * (-np.log(10000.0) / D))
    pe[:, 0::2] = np.sin(position * div_term)
    pe[:, 1::2] = np.cos(position * div_term)
    return pe


def shape_constants():
    bfloat16 = mybir.dt.np(BF16)
    ident = np.eye(P, dtype=np.float32)
    mask = np.where(np.arange(P)[None, :] > np.arange(P)[:, None], MASKED, 0.0).astype(np.float32)
    pick = np.zeros((HEADS, KT, P), np.float32)
    for hd in range(HEADS):
        pick[hd, hd // HT, DK * (hd % HT):DK * (hd % HT) + DK] = 1.0
    sel = np.zeros((PARTS * E, E, P), np.float32)
    for e in range(E):
        sel[e::E, e, :] = 0.5
    return ident, ident.astype(bfloat16), mask.astype(bfloat16), pick, sel.astype(bfloat16)


def kernel(x, L0_tok_weight, L0_tok_gamma, L0_tok_beta, L0_attn_Wq, L0_attn_bq, L0_attn_Wk, L0_attn_bk,
           L0_attn_Wv, L0_attn_bv, L0_attn_Wo, L0_attn_bo, L0_ffn_router_w, L0_ffn_w_gate, L0_ffn_w_up,
           L0_ffn_w_down, L0_ffn_ws_gate, L0_ffn_ws_up, L0_ffn_ws_down):
    import concourse.bacc as bacc
    from concourse.bass_utils import run_bass_kernel_spmd

    ident, ident16, mask, pick, sel = shape_constants()
    c = np.ascontiguousarray
    arrays = {
        "ids": c(np.asarray(x).T), "table": L0_tok_weight, "base_pe": base_pe_table(),
        "gamma": L0_tok_gamma, "beta": L0_tok_beta,
        "wq": c(np.asarray(L0_attn_Wq).T), "bq": c(np.asarray(L0_attn_bq).reshape(KT, P).T), "wk": c(np.asarray(L0_attn_Wk).T), "bk": c(np.asarray(L0_attn_bk).reshape(KT, P).T),
        "wv": c(np.asarray(L0_attn_Wv).T), "bv": L0_attn_bv, "wo": c(np.asarray(L0_attn_Wo).T), "bo": L0_attn_bo,
        "router": L0_ffn_router_w, "gate": L0_ffn_w_gate, "up": L0_ffn_w_up, "down": L0_ffn_w_down,
        "s_gate": L0_ffn_ws_gate, "s_up": L0_ffn_ws_up, "s_down": L0_ffn_ws_down,
        "ident": ident, "ident16": ident16, "mask": mask, "pick": pick, "sel": sel,
    }
    nc = bacc.Bacc("TRN2", target_bir_lowering=False, num_devices=1)
    feeds, args = {}, []
    for name, a in arrays.items():
        a = c(a)
        feeds[f"in_{name}"] = a
        args.append(nc.dram_tensor(f"in_{name}", a.shape, mybir.dt.from_np(a.dtype), kind="ExternalInput").ap())
    shape = (x.shape[0], SEQ, D)
    args.append(nc.dram_tensor("out", shape, F32, kind="ExternalOutput").ap())
    build(nc, *args)
    r = run_bass_kernel_spmd(nc, [feeds], core_ids=[0])
    return r.results[0]["out"]
```
